# Optimizing a Trainium2 kernel written in Bass

```python
import numpy as np
import jax
import jax.numpy as jnp

def _softmax(x, axis=-1):
    return jax.nn.softmax(x, axis=axis)

def _gelu(x):
    return jax.nn.gelu(x, approximate=True)

def _silu(x):
    return jax.nn.silu(x)

def _sigmoid(x):
    return jax.nn.sigmoid(x)

def _layernorm(x, axis=-1, eps=1e-05):
    m = jnp.mean(x, axis=axis, keepdims=True)
    v = jnp.var(x, axis=axis, keepdims=True)
    return (x - m) / jnp.sqrt(v + eps)

def _scatter_add(tgt, idx, src, axis=0):
    return tgt.at[idx].add(src)

def _segment_sum(src, seg, n):
    return jax.ops.segment_sum(src, seg, n)
kernel_name = 'mk_cond_seq_d2_seqx_r4_9d95fd'

def setup_inputs(seed: int=0):
    np.random.seed(seed)
    _w = jnp.asarray

    def _rec_inputs():
        import jax
        import jax.numpy as jnp
        _rk = jax.random.key(seed)
        x = -0.0002928 + 1 * jax.random.normal(jax.random.fold_in(_rk, 1), (8, 512, 256), jnp.float32)
        _lenS = 512 - jax.random.randint(jax.random.fold_in(_rk, 7), (8,), 0, max(1, 512 // 4) + 1, jnp.int32)
        _lenS2 = 512 - jax.random.randint(jax.random.fold_in(_rk, 8), (8,), 0, max(1, 512 // 4) + 1, jnp.int32)
        cond_1024 = 0.00786388 + 1.0143 * jax.random.normal(jax.random.fold_in(_rk, 11), (8, 256), jnp.float32)
        _validS = jnp.arange(512)[None, :] < _lenS[:, None]
        _validS2 = jnp.arange(512)[None, :] < _lenS2[:, None]
        _causal = jnp.tril(jnp.ones((512, 512), dtype=bool))
        mask_BxS_bf1 = jnp.ones((8, 512), dtype=bool)
        mask_BxS_bk0 = jnp.logical_not(jnp.broadcast_to(_validS[:, :], (8, 512)))
        return (x, cond_1024, mask_BxS_bf1, mask_BxS_bk0)
    x, cond_1024, mask_BxS_bf1, mask_BxS_bk0 = _rec_inputs()

    def _L0_cond_setup():
        import jax, jax.numpy as jnp
        import numpy as np
        EPS = 1e-05
        NEG_INF = -1e+30

        def layer_norm(x, g, b):
            mu = jnp.mean(x, axis=-1, keepdims=True)
            var = jnp.var(x, axis=-1, keepdims=True)
            return (x - mu) * jax.lax.rsqrt(var + EPS) * g + b
        B, L, D, H, F = (2, 512, 256, 16, 1024)
        key = jax.random.key(seed)
        ks = jax.random.split(key, 12)
        s = 0.02
        return {'x': jax.random.normal(ks[0], (B, L, D), jnp.float32), 'torus_dist': jax.random.uniform(ks[1], (1, L, L), jnp.float32), 'time_emb': jax.random.normal(ks[2], (B, D), jnp.float32), 'mask': jnp.ones((B, L), dtype=bool), 'ln1_g': jnp.ones((D,), jnp.float32), 'ln1_b': jnp.zeros((D,), jnp.float32), 'Wqkv': jax.random.normal(ks[3], (D, 3 * D), jnp.float32) * s, 'Wout': jax.random.normal(ks[4], (D, D), jnp.float32) * s, 'torus_scale': jnp.full((H,), 0.1, jnp.float32), 'ln2_g': jnp.ones((D,), jnp.float32), 'ln2_b': jnp.zeros((D,), jnp.float32), 'W1': jax.random.normal(ks[5], (D, F), jnp.float32) * s, 'b1': jnp.zeros((F,), jnp.float32), 'W2': jax.random.normal(ks[6], (F, D), jnp.float32) * s, 'b2': jnp.zeros((D,), jnp.float32), 'Wt': jax.random.normal(ks[7], (D, 2 * D), jnp.float32) * s, 'bt': jnp.zeros((2 * D,), jnp.float32)}
    _L0_cond_all = _L0_cond_setup()
    _L0_cond_in = {k: v for k, v in _L0_cond_all.items() if k in ('torus_dist', 'ln1_g', 'ln1_b', 'Wqkv', 'Wout', 'torus_scale', 'ln2_g', 'ln2_b', 'W1', 'b1', 'W2', 'b2', 'Wt', 'bt')}
    del _L0_cond_all

    def _L1_cond_setup():
        import jax, jax.numpy as jnp
        import numpy as np
        B, N, C = (4, 256, 256)
        H = 16
        D = C // H
        FF = 4 * C
        EPS = 1e-05

        def _layernorm(x):
            mu = jnp.mean(x, axis=-1, keepdims=True)
            var = jnp.mean(jnp.square(x - mu), axis=-1, keepdims=True)
            return (x - mu) * jax.lax.rsqrt(var + EPS)

        def _modulate(x, shift, scale):
            return x * (1.0 + scale[:, None, :]) + shift[:, None, :]

        def _attention(x, node_mask, qkv_w, proj_w, proj_b):
            b, n, c = x.shape
            qkv = (x @ qkv_w).reshape(b, n, 3, H, D)
            q, k, v = jnp.moveaxis(qkv, 2, 0)
            q = q.transpose(0, 2, 1, 3)
            k = k.transpose(0, 2, 1, 3)
            v = v.transpose(0, 2, 1, 3)
            scale = D ** (-0.5)
            scores = jnp.einsum('bhnd,bhmd->bhnm', q, k) * scale
            mask = node_mask[:, None, None, :]
            scores = jnp.where(mask, scores, -jnp.inf)
            attn = jax.nn.softmax(scores, axis=-1)
            out = jnp.einsum('bhnm,bhmd->bhnd', attn, v)
            out = out.transpose(0, 2, 1, 3).reshape(b, n, c)
            return out @ proj_w + proj_b

        def _mlp(x, fc1_w, fc1_b, fc2_w, fc2_b):
            h = jax.nn.gelu(x @ fc1_w + fc1_b, approximate=False)
            return h @ fc2_w + fc2_b
        key = jax.random.key(seed)
        ks = jax.random.split(key, 16)
        s = 0.02
        return {'x': jax.random.normal(ks[0], (B, N, C), jnp.float32), 'c': jax.random.normal(ks[1], (B, C), jnp.float32), 'node_mask': jax.random.randint(ks[2], (B, N), 0, 2) > 0, 'qkv_w': jax.random.normal(ks[3], (C, 3 * C), jnp.float32) * s, 'proj_w': jax.random.normal(ks[4], (C, C), jnp.float32) * s, 'proj_b': jnp.zeros((C,), jnp.float32), 'fc1_w': jax.random.normal(ks[5], (C, FF), jnp.float32) * s, 'fc1_b': jnp.zeros((FF,), jnp.float32), 'fc2_w': jax.random.normal(ks[6], (FF, C), jnp.float32) * s, 'fc2_b': jnp.zeros((C,), jnp.float32), 'ada1_w': jax.random.normal(ks[7], (C, C), jnp.float32) * s, 'ada1_b': jnp.zeros((C,), jnp.float32), 'ada2_w': jax.random.normal(ks[8], (C, 6 * C), jnp.float32) * s, 'ada2_b': jnp.zeros((6 * C,), jnp.float32)}
    _L1_cond_all = _L1_cond_setup()
    _L1_cond_in = {k: v for k, v in _L1_cond_all.items() if k in ('qkv_w', 'proj_w', 'proj_b', 'fc1_w', 'fc1_b', 'fc2_w', 'fc2_b', 'ada1_w', 'ada1_b', 'ada2_w', 'ada2_b')}
    del _L1_cond_all
    return {'x': x, 'cond_1024': cond_1024, 'mask_BxS_bf1': mask_BxS_bf1, 'mask_BxS_bk0': mask_BxS_bk0, 'L0_cond_torus_dist': _L0_cond_in['torus_dist'], 'L0_cond_ln1_g': _L0_cond_in['ln1_g'], 'L0_cond_ln1_b': _L0_cond_in['ln1_b'], 'L0_cond_Wqkv': _L0_cond_in['Wqkv'], 'L0_cond_Wout': _L0_cond_in['Wout'], 'L0_cond_torus_scale': _L0_cond_in['torus_scale'], 'L0_cond_ln2_g': _L0_cond_in['ln2_g'], 'L0_cond_ln2_b': _L0_cond_in['ln2_b'], 'L0_cond_W1': _L0_cond_in['W1'], 'L0_cond_b1': _L0_cond_in['b1'], 'L0_cond_W2': _L0_cond_in['W2'], 'L0_cond_b2': _L0_cond_in['b2'], 'L0_cond_Wt': _L0_cond_in['Wt'], 'L0_cond_bt': _L0_cond_in['bt'], 'L1_cond_qkv_w': _L1_cond_in['qkv_w'], 'L1_cond_proj_w': _L1_cond_in['proj_w'], 'L1_cond_proj_b': _L1_cond_in['proj_b'], 'L1_cond_fc1_w': _L1_cond_in['fc1_w'], 'L1_cond_fc1_b': _L1_cond_in['fc1_b'], 'L1_cond_fc2_w': _L1_cond_in['fc2_w'], 'L1_cond_fc2_b': _L1_cond_in['fc2_b'], 'L1_cond_ada1_w': _L1_cond_in['ada1_w'], 'L1_cond_ada1_b': _L1_cond_in['ada1_b'], 'L1_cond_ada2_w': _L1_cond_in['ada2_w'], 'L1_cond_ada2_b': _L1_cond_in['ada2_b']}

def reference(x, cond_1024, mask_BxS_bf1, mask_BxS_bk0, L0_cond_torus_dist, L0_cond_ln1_g, L0_cond_ln1_b, L0_cond_Wqkv, L0_cond_Wout, L0_cond_torus_scale, L0_cond_ln2_g, L0_cond_ln2_b, L0_cond_W1, L0_cond_b1, L0_cond_W2, L0_cond_b2, L0_cond_Wt, L0_cond_bt, L1_cond_qkv_w, L1_cond_proj_w, L1_cond_proj_b, L1_cond_fc1_w, L1_cond_fc1_b, L1_cond_fc2_w, L1_cond_fc2_b, L1_cond_ada1_w, L1_cond_ada1_b, L1_cond_ada2_w, L1_cond_ada2_b):
    import jax
    import jax.numpy as jnp

    def _L0_cond_ref(x, torus_dist, time_emb, mask, ln1_g, ln1_b, Wqkv, Wout, torus_scale, ln2_g, ln2_b, W1, b1, W2, b2, Wt, bt):
        import jax, jax.numpy as jnp
        import numpy as np
        EPS = 1e-05
        NEG_INF = -1e+30

        def layer_norm(x, g, b):
            mu = jnp.mean(x, axis=-1, keepdims=True)
            var = jnp.var(x, axis=-1, keepdims=True)
            return (x - mu) * jax.lax.rsqrt(var + EPS) * g + b
        B, L, D = x.shape
        H = torus_scale.shape[0]
        hd = D // H
        tp = jax.nn.gelu(time_emb) @ Wt + bt
        scale, shift = jnp.split(tp, 2, axis=-1)
        h = layer_norm(x, ln1_g, ln1_b) * (1.0 + scale[:, None, :]) + shift[:, None, :]
        qkv = (h @ Wqkv).reshape(B, L, 3, H, hd)
        q = jnp.transpose(qkv[:, :, 0], (0, 2, 1, 3))
        k = jnp.transpose(qkv[:, :, 1], (0, 2, 1, 3))
        v = jnp.transpose(qkv[:, :, 2], (0, 2, 1, 3))
        scores = jnp.einsum('bhqd,bhkd->bhqk', q, k) / np.sqrt(hd).astype(np.float32)
        scores = scores - torus_dist[:, None, :, :] * torus_scale[None, :, None, None]
        pad = ~mask[:, None, None, :]
        scores = jnp.where(pad, NEG_INF, scores)
        attn = jax.nn.softmax(scores, axis=-1)
        attn = jnp.nan_to_num(attn, nan=0.0)
        out = jnp.einsum('bhqk,bhkd->bhqd', attn, v)
        out = jnp.transpose(out, (0, 2, 1, 3)).reshape(B, L, D)
        x = x + out @ Wout
        h2 = layer_norm(x, ln2_g, ln2_b)
        x = x + (jax.nn.gelu(h2 @ W1 + b1) @ W2 + b2)
        return x

    def _L1_cond_ref(x, c, node_mask, qkv_w, proj_w, proj_b, fc1_w, fc1_b, fc2_w, fc2_b, ada1_w, ada1_b, ada2_w, ada2_b):
        import jax, jax.numpy as jnp
        import numpy as np
        B, N, C = (4, 256, 256)
        H = 16
        D = C // H
        FF = 4 * C
        EPS = 1e-05

        def _layernorm(x):
            mu = jnp.mean(x, axis=-1, keepdims=True)
            var = jnp.mean(jnp.square(x - mu), axis=-1, keepdims=True)
            return (x - mu) * jax.lax.rsqrt(var + EPS)

        def _modulate(x, shift, scale):
            return x * (1.0 + scale[:, None, :]) + shift[:, None, :]

        def _attention(x, node_mask, qkv_w, proj_w, proj_b):
            b, n, c = x.shape
            qkv = (x @ qkv_w).reshape(b, n, 3, H, D)
            q, k, v = jnp.moveaxis(qkv, 2, 0)
            q = q.transpose(0, 2, 1, 3)
            k = k.transpose(0, 2, 1, 3)
            v = v.transpose(0, 2, 1, 3)
            scale = D ** (-0.5)
            scores = jnp.einsum('bhnd,bhmd->bhnm', q, k) * scale
            mask = node_mask[:, None, None, :]
            scores = jnp.where(mask, scores, -jnp.inf)
            attn = jax.nn.softmax(scores, axis=-1)
            out = jnp.einsum('bhnm,bhmd->bhnd', attn, v)
            out = out.transpose(0, 2, 1, 3).reshape(b, n, c)
            return out @ proj_w + proj_b

        def _mlp(x, fc1_w, fc1_b, fc2_w, fc2_b):
            h = jax.nn.gelu(x @ fc1_w + fc1_b, approximate=False)
            return h @ fc2_w + fc2_b
        ada = jax.nn.silu(c @ ada1_w + ada1_b) @ ada2_w + ada2_b
        shift_msa, scale_msa, gate_msa, shift_mlp, scale_mlp, gate_mlp = jnp.split(ada, 6, axis=1)
        attn_out = _attention(x, node_mask, qkv_w, proj_w, proj_b)
        x = x + gate_msa[:, None, :] * _modulate(_layernorm(attn_out), shift_msa, scale_msa)
        mlp_out = _mlp(x, fc1_w, fc1_b, fc2_w, fc2_b)
        x = x + gate_mlp[:, None, :] * _modulate(_layernorm(mlp_out), shift_mlp, scale_mlp)
        return x
    x = _L0_cond_ref(x, L0_cond_torus_dist, cond_1024, mask_BxS_bf1, L0_cond_ln1_g, L0_cond_ln1_b, L0_cond_Wqkv, L0_cond_Wout, L0_cond_torus_scale, L0_cond_ln2_g, L0_cond_ln2_b, L0_cond_W1, L0_cond_b1, L0_cond_W2, L0_cond_b2, L0_cond_Wt, L0_cond_bt)
    x = _L1_cond_ref(x, cond_1024, mask_BxS_bk0, L1_cond_qkv_w, L1_cond_proj_w, L1_cond_proj_b, L1_cond_fc1_w, L1_cond_fc1_b, L1_cond_fc2_w, L1_cond_fc2_b, L1_cond_ada1_w, L1_cond_ada1_b, L1_cond_ada2_w, L1_cond_ada2_b)
    return x

_drawn_inputs = setup_inputs


def setup_inputs(seed=0):
    import zlib

    import numpy as np

    out = dict(_drawn_inputs(seed))
    spreads = {'L0_cond_ln1_g': (1.0, 0.6),
     'L0_cond_ln1_b': (0.0, 0.753),
     'L0_cond_torus_scale': (0.10000000149011612, 0.6),
     'L0_cond_ln2_g': (1.0, 0.6),
     'L0_cond_ln2_b': (0.0, 0.772),
     'L0_cond_b1': (0.0, 0.1),
     'L0_cond_b2': (0.0, 0.1),
     'L0_cond_bt': (0.0, 0.8),
     'L1_cond_proj_b': (0.0, 0.1),
     'L1_cond_fc1_b': (0.0, 0.346),
     'L1_cond_fc2_b': (0.0, 0.1),
     'L1_cond_ada1_b': (0.0, 0.358),
     'L1_cond_ada2_b': (0.0, 0.1)}
    factors = {'L0_cond_torus_dist': 64.0, 'L0_cond_Wt': 2.748}
    for name, (base, spread) in spreads.items():
        noise = np.random.default_rng([zlib.crc32(name.encode()), seed]).standard_normal(out[name].shape)
        drawn = base * np.exp(spread * noise) if base else spread * noise
        out[name] = jnp.asarray(drawn.astype(out[name].dtype))
    for name, factor in factors.items():
        out[name] = (out[name] * factor).astype(out[name].dtype)
    return out
```

```python
from contextlib import ExitStack

import concourse.bass as bass
from concourse import mybir

ALU = mybir.AluOpType
ACT = mybir.ActivationFunctionType
F32 = mybir.dt.float32
F32R = mybir.dt.float32r
U8 = mybir.dt.uint8

P = 128
EPS = 1e-5
PAD = 1e30
QUERY_SCALE = 0.25


def build(nc, d, out):
    B, L, D = d["x"].shape
    H = d["L0_cond_torus_scale"].shape[0]
    F = d["L0_cond_W1"].shape[1]
    HD = D // H
    TT = L // P
    DC = D // P
    FCH = F // P
    HG = 4
    G = H // HG
    SLOT = P // HG
    KROWS = 4 * HD
    UNITS = 2 * H
    HALF = L // 2
    GQ = 2 * G
    TILES = 2 * UNITS
    assert HD == 16 and TT == 4 and DC == 2 and G == 4

    ITEMS = ([("t1", i) for i in range(DC)] + [("qk", i) for i in range(4)] + [("v", i) for i in range(TT)]
             + [("wout", i) for i in range(TT)] + [("t2", i) for i in range(DC)]
             + [("up", i) for i in range(FCH)] + [("down", i) for i in range(TT)])
    ITEM = {name: n for n, name in enumerate(ITEMS)}
    ND = len(ITEMS)
    assert ND % 2 == 0

    with ExitStack() as ctx:
        def sb(name, shape, dt=F32):
            return ctx.enter_context(nc.sbuf_tensor(name, shape, dt))

        def sem(name):
            return ctx.enter_context(nc.semaphore(name))

        def dram(name, shape):
            return nc.dram_tensor(name, shape, F32, kind="Internal").ap()

        x_mid = dram("x_mid", (B, L, D))
        qk_halves = dram("qk_halves", (2, B, 2, 2, D, L))
        mod_rows = dram("mod_rows", (B, 4 * D))

        score_bank = [ctx.enter_context(nc.psum_tensor(f"score{i}", [P, L], F32)) for i in range(2)]
        turned_bank = [ctx.enter_context(nc.psum_tensor(f"turned{i}", [P, L], F32)) for i in range(2)]
        pv_bank = ctx.enter_context(nc.psum_tensor("pv", [P, L], F32))
        den_bank = ctx.enter_context(nc.psum_tensor("den", [P, L], F32))
        dense_bank = [ctx.enter_context(nc.psum_tensor(f"dense{i}", [P, L], F32)) for i in range(2)]

        w_qkv = sb("w_qkv", [P, DC, 3 * D])
        w_out = sb("w_out", [P, G, D])
        w_up = sb("w_up", [P, DC, F])
        w_down = sb("w_down", [P, FCH, D])
        up_bias = sb("up_bias", [P, FCH])
        down_bias = sb("down_bias", [P, D])
        ident = sb("ident", [P, P])
        den_select = sb("den_select", [P, P])
        minus_half = sb("minus_half", [P, TT])
        neg_scale = sb("neg_scale", [P, H])
        dist = sb("dist", [P, TT, L])
        no_bias = sb("no_bias", [P, L])
        ln2_gb = sb("ln2_gb", [P, 2, DC])
        ab = sb("ab", [P, 2, DC, B])
        x_in_t = sb("x_in_t", [P, TT, D])
        x_res = sb("x_res", [P, TT, D])
        x_norm = sb("x_norm", [P, TT, D])
        x_mid_t = sb("x_mid_t", [P, TT, D])
        branch = sb("branch", [P, TT, D])
        y_t = sb("y_t", [P, TT, D])
        mod = sb("mod", [P, 4, D])
        feat = sb("feat", [P, DC, L])
        qk_high = sb("qk_high", [P, 4, L], F32R)
        qk_low = sb("qk_low", [P, 4, L], F32R)
        q_rows = sb("q_rows", [KROWS + 1, 2, HG, L], F32R)
        k_rows = sb("k_rows", [KROWS + 1, 2, HG, L], F32R)
        v_ext = sb("v_ext", [P, TT, H, SLOT])
        bias = sb("bias", [P, 2, 2, L])
        shifted = sb("shifted", [P, 2, 2, L])
        probs = sb("probs", [P, 8, TT, HALF])
        head_out = sb("head_out", [P, 2, HALF])
        inv_sum = sb("inv_sum", [P, HALF])
        attn = sb("attn", [P, G, L])
        hidden = sb("hidden", [P, FCH, L])
        row_max = sb("row_max", [P, 4])
        stats = sb("stats", [P, TT, 6])
        mean_var = sb("mean_var", [P, TT, 2])
        var_eps = sb("var_eps", [P, TT])
        rstd = sb("rstd", [P, TT])
        mask_row = sb("mask_row", [KROWS + 1, L], U8)
        mask_neg = sb("mask_neg", [KROWS + 1, L], F32R)
        mask_col = sb("mask_col", [P, TT], U8)
        mask_colf = sb("mask_colf", [P, TT])
        cond_t = sb("cond_t", [P, DC, B])
        cond_g = sb("cond_g", [P, DC, B])
        u_t = sb("u_t", [P, DC, B])
        tp = sb("tp", [P, 4, B])
        bt_col = sb("bt_col", [P, 4])
        ada1_col = sb("ada1_col", [P, DC])
        ln1_gb = sb("ln1_gb", [P, 2, DC])
        early = probs[:, :, :, :].rearrange("p a b c -> p (a b c)")
        ada2 = early[:, 0:3072].rearrange("p (c n) -> p c n", c=DC)
        w_t = early[:, 3072:4096].rearrange("p (c n) -> p c n", c=DC)
        ada1 = early[:, 4096:4608].rearrange("p (c n) -> p c n", c=DC)
        ada2_bias = early[0:B, 4608:6144]
        ada = early[0:B, 6144:7680]
        mod_out = hidden[0:B, 0:2, :].rearrange("p a b -> p (a b)")

        small_loaded = sem("small_loaded")
        w_loaded = sem("w_loaded")
        pool_consts = sem("pool_consts")
        dve_consts = sem("dve_consts")
        cond_ready = sem("cond_ready")
        tp_ready = sem("tp_ready")
        silu_ready = sem("silu_ready")
        ada_ready = sem("ada_ready")
        setup_step = sem("setup_step")
        mod_stored = sem("mod_stored")
        setup_done = sem("setup_done")
        carried = sem("carried")
        S = []
        for blk in range(2):
            n = {}
            for name in ("x_loaded", "res_loaded", "mask_loaded", "mask_ready", "col_ready", "vmask_ready",
                         "mod_loaded", "halves_stored0", "halves_stored1", "base_free", "group0_loaded", "group1_loaded",
                         "group_used", "scores_ready", "scores_used", "bias_ready", "bias_used", "shifted_ready",
                         "shifted_used", "turned_ready", "probs_ready", "probs_used", "pv_ready",
                         "head_out_ready", "den_ready", "inv_ready", "attn_ready", "attn_used", "dense_ready",
                         "dense_used0", "dense_used1", "high_ready", "stats_ready", "mean_ready", "var_ready",
                         "rstd_ready", "norm_ready", "mid_ready", "res_ready", "chain", "y_ready", "y_stored"):
                n[name] = sem(f"b{blk}_{name}")
            S.append(n)

        def after(eng, s, b, per_batch, n):
            eng.wait_ge(s, b * per_batch + n)

        def after_alone(eng, s, b, per_batch, n):
            eng.wait_ge(s, b * per_batch + n)
            eng.sem_inc(carried, 1)

        def bank_free(eng, s, b, k):
            after(eng, (s["dense_used0"], s["dense_used1"])[k % 2], b, ND // 2, k // 2 + 1)

        def item_read(eng, s, b, k):
            after(eng, (s["dense_used0"], s["dense_used1"])[k % 2], b, ND // 2, k // 2 + 2)

        def used(s, k):
            return (s["dense_used0"], s["dense_used1"])[k % 2]

        block = ctx.enter_context(nc.Block())
        W_COUNT = {}

        @block.sync
        def _(sp):
            n_loads = 0

            def load_small(dst, src):
                sp.dma_start(dst, src).then_inc(small_loaded, 16)

            def load(dst, src):
                nonlocal n_loads
                sp.dma_start(dst, src).then_inc(w_loaded, 16)
                n_loads += 1

            def load_weights(pre, qkv, wout, up, up_b, down, down_b):
                load(w_qkv[:, :, :], d[pre + qkv].rearrange("(c p) n -> p c n", p=P))
                for j in range(HG):
                    load(w_out[SLOT * j:SLOT * j + HD, :, :],
                         d[pre + wout].rearrange("(g j e) n -> j e g n", j=HG, e=HD)[j])
                load(w_up[:, :, :], d[pre + up].rearrange("(c p) n -> p c n", p=P))
                load(w_down[:, :, :], d[pre + down].rearrange("(c p) n -> p c n", p=P))
                load(up_bias[:, :], d[pre + up_b].rearrange("(c p) -> p c", p=P))
                load(down_bias[:, :], d[pre + down_b].unsqueeze(0).broadcast_to([P, D]))

            with nc.allow_non_contiguous_dma(reason="small vectors laid on partitions"):
                load_small(cond_t[:, 0, :], d["cond_1024"][:, 0:P].rearrange("b p -> p b"))
                load_small(cond_t[:, 1, :], d["cond_1024"][:, P:D].rearrange("b p -> p b"))
                load_small(w_t, d["L0_cond_Wt"].rearrange("(c p) n -> p c n", p=P))
                load_small(bt_col[:, :], d["L0_cond_bt"].rearrange("(c p) -> p c", p=P))
                load_small(ln1_gb[:, 0, :], d["L0_cond_ln1_g"].rearrange("(c p) -> p c", p=P))
                load_small(ln1_gb[:, 1, :], d["L0_cond_ln1_b"].rearrange("(c p) -> p c", p=P))
                load_small(ln2_gb[:, 0, :], d["L0_cond_ln2_g"].rearrange("(c p) -> p c", p=P))
                load_small(ln2_gb[:, 1, :], d["L0_cond_ln2_b"].rearrange("(c p) -> p c", p=P))
                load_small(ada1, d["L1_cond_ada1_w"].rearrange("(c p) n -> p c n", p=P))
                load_small(ada1_col[:, :], d["L1_cond_ada1_b"].rearrange("(c p) -> p c", p=P))
                load_small(ada2, d["L1_cond_ada2_w"].rearrange("(c p) n -> p c n", p=P))
                load_small(ada2_bias, d["L1_cond_ada2_b"].unsqueeze(0).broadcast_to([B, 6 * D]))
                load_small(neg_scale[:, :], d["L0_cond_torus_scale"].unsqueeze(0).broadcast_to([P, H]))
                load_small(dist[:, :, :], d["L0_cond_torus_dist"][0].rearrange("(t p) k -> p t k", p=P))
                sp.wait_ge(dve_consts, DVE_CONSTS)
                sp.wait_ge(pool_consts, POOL_CONSTS)
                load_weights("L0_cond_", "Wqkv", "Wout", "W1", "b1", "W2", "b2")
                W_COUNT[0] = 16 * n_loads
                sp.wait_ge(setup_step, SETUP_STEPS)
                sp.dma_start(mod_rows, mod_out).then_inc(mod_stored, 16)
                sp.wait_ge(mod_stored, 16)
                sp.sem_inc(setup_done, 1)

                for blk, s in enumerate(S):
                    x_src = (d["x"], x_mid)[blk]
                    y_dst = (x_mid, out)[blk]
                    mask = (d["mask_BxS_bf1"], d["mask_BxS_bk0"])[blk]

                    def load_x(b, s=s, x_src=x_src):
                        sp.dma_start(x_in_t[:, :, :], x_src[b].rearrange("(t p) n -> p t n", p=P))\
                            .then_inc(s["x_loaded"], 16)

                    def load_res(b, s=s, x_src=x_src):
                        sp.dma_start(x_res[:, :, :], x_src[b].rearrange("(t p) n -> p t n", p=P))\
                            .then_inc(s["res_loaded"], 16)

                    def load_mod(b, s=s):
                        sp.dma_start(mod[:, :, :].rearrange("p a n -> p (a n)"),
                                     mod_rows[b].unsqueeze(0).broadcast_to([P, 4 * D])).then_inc(s["mod_loaded"], 16)

                    if blk == 1:
                        sp.wait_ge(S[0]["y_stored"], 16 * (B + 1))
                        load_weights("L1_cond_", "qkv_w", "proj_w", "fc1_w", "fc1_b", "fc2_w", "fc2_b")
                        load(w_out[HD:HD + 1, 0, :], d["L1_cond_proj_b"].unsqueeze(0))
                        W_COUNT[1] = 16 * n_loads
                        load_mod(0)
                    load_x(0)
                    if blk == 0:
                        load_res(0)
                    with sp.Fori(0, B) as b:
                        sp.dma_start(mask_row[KROWS:KROWS + 1, :], mask[bass.ds(b, 1), :])\
                            .then_inc(s["mask_loaded"], 16)
                        if blk == 1:
                            sp.dma_start(mask_col[:, :], mask[b].rearrange("(t p) -> p t", p=P))\
                                .then_inc(s["mask_loaded"], 16)
                        for c in range(4):
                            item_read(sp, s, b, ITEM["qk", c])
                            sp.sem_inc(carried, 1)
                            rows = slice(P * (c // 2), P * (c // 2) + P)
                            stored = (s["halves_stored0"], s["halves_stored1"])[c // 2]
                            sp.dma_start(qk_halves[blk, b, 0, c % 2, rows, :], qk_high[:, c, :].bitcast(F32))\
                                .then_inc(stored, 16)
                            sp.dma_start(qk_halves[blk, b, 1, c % 2, rows, :], qk_low[:, c, :].bitcast(F32))\
                                .then_inc(stored, 16)
                        for g in range(G):
                            if g % 2 == 0:
                                after_alone(sp, (s["halves_stored0"], s["halves_stored1"])[g // 2], b, 64, 64)
                            if g == G - 1:
                                sp.sem_inc(s["base_free"], 1)
                            if g == 0:
                                after_alone(sp, s["mask_ready"], b, 1, 1)
                            after_alone(sp, s["group_used"], b, G, g + 1)
                            loaded = (s["group0_loaded"], s["group1_loaded"])[g % 2]
                            rows = slice(HG * HD * g, HG * HD * (g + 1))
                            for r in range(4):
                                sp.dma_start(q_rows[HD * r:HD * r + HD, g % 2, :, :].bitcast(F32),
                                             qk_halves[blk, b, r // 2, 0, rows, :]
                                             .rearrange("(h e) n -> e h n", e=HD)).then_inc(loaded, 16)
                                sp.dma_start(k_rows[HD * r:HD * r + HD, g % 2, :, :].bitcast(F32),
                                             qk_halves[blk, b, r % 2, 1, rows, :]
                                             .rearrange("(h e) n -> e h n", e=HD)).then_inc(loaded, 16)
                            sp.dma_start(k_rows[KROWS:KROWS + 1, g % 2, :, :].bitcast(F32),
                                         mask_neg[KROWS:KROWS + 1, :].bitcast(F32).unsqueeze(1)
                                         .broadcast_to([1, HG, L])).then_inc(loaded, 16)
                            if g == 1:
                                nxt = (b + 1) % B
                                if blk == 0:
                                    after_alone(sp, s["norm_ready"], b, 2, 1)
                                else:
                                    after_alone(sp, s["dense_ready"], b, ND, DC)
                                    after_alone(sp, s["res_ready"], b, 2, 1)
                                load_x(nxt)
                        if blk == 0:
                            after_alone(sp, s["mid_ready"], b, 1, 1)
                            load_res(nxt)
                        after_alone(sp, s["y_ready"], b, 1, 1)
                        sp.dma_start(y_dst[b].rearrange("(t p) n -> p t n", p=P), y_t[:, :, :])\
                            .then_inc(s["y_stored"], 16)
                        if blk == 1:
                            load_mod(nxt)
                sp.wait_ge(S[1]["y_stored"], 16 * (B + 1))
                sp.wait_ge(S[1]["mod_loaded"], 16 * (B + 1))
                sp.wait_ge(S[1]["x_loaded"], 16 * (B + 1))
                sp.wait_ge(S[0]["res_loaded"], 16 * (B + 1))

        @block.gpsimd
        def _(pool):
            pool.memset(ident[:, :], 0.0).then_inc(pool_consts, 1)
            pool.memset(den_select[:, :], 0.0).then_inc(pool_consts, 1)
            pool.memset(minus_half[:, :], -0.5).then_inc(pool_consts, 1)
            pool.wait_ge(pool_consts, 2)
            pool.affine_select(out=ident[:, :], in_=ident[:, :], compare_op=ALU.not_equal, fill=1.0, base=0,
                               pattern=[[-1, P]], channel_multiplier=1).then_inc(pool_consts, 1)
            sel = den_select[:, :].rearrange("p (a c) -> p a c", a=HG)
            pool.affine_select(out=sel, in_=sel, compare_op=ALU.not_equal, fill=1.0, base=-HD,
                               pattern=[[-SLOT, HG], [0, SLOT]], channel_multiplier=1).then_inc(pool_consts, 1)

            for blk, s in enumerate(S):
                def inverse_std(b, n, s=s):
                    after_alone(pool, s["mean_ready"], b, 2, n + 1)
                    pool.tensor_scalar_add(var_eps[:, :], mean_var[:, :, 1], EPS).then_inc(s["var_ready"], 1)
                    after(pool, s["var_ready"], b, 2, n + 1)
                    pool.tensor_tensor(rstd[:, :], var_eps[:, :], minus_half[:, :], ALU.pow).then_inc(s["rstd_ready"], 1)

                with pool.Fori(0, B) as b:
                    after_alone(pool, s["mask_loaded"], b, 16 + 16 * blk, 16 + 16 * blk)
                    pool.tensor_scalar(mask_neg[KROWS:KROWS + 1, :], mask_row[KROWS:KROWS + 1, :], PAD, -PAD,
                                       ALU.mult, ALU.add).then_inc(s["mask_ready"], 1)
                    after_alone(pool, s["mask_ready"], b, 1, 1)
                    if blk == 0:
                        inverse_std(b, 0)
                        inverse_std(b, 1)
                        after(pool, s["norm_ready"], b, 2, 2)
                        pool.tensor_tensor(x_mid_t[:, :, :], x_mid_t[:, :, :],
                                           down_bias[:, :].unsqueeze(1).broadcast_to([P, TT, D]), ALU.add)\
                            .then_inc(s["res_ready"], 1)
                    else:
                        pool.tensor_copy(mask_colf[:, :], mask_col[:, :]).then_inc(s["col_ready"], 1)
                        after_alone(pool, s["col_ready"], b, 1, 1)
                        after_alone(pool, s["probs_used"], b, GQ, 2)
                        pool.tensor_copy(v_ext[:, :, :, HD],
                                         mask_colf[:, :].unsqueeze(2).broadcast_to([P, TT, H]))\
                            .then_inc(s["vmask_ready"], 1)
                        after(pool, s["x_loaded"], b, 16, 16)
                        after(pool, s["mod_loaded"], b, 16, 16)
                        after(pool, s["chain"], b, 4, 1)
                        pool.tensor_tensor(x_res[:, :, :], x_in_t[:, :, :],
                                           mod[:, 1:2, :].broadcast_to([P, TT, D]), ALU.add).then_inc(s["res_ready"], 1)
                        inverse_std(b, 0)
                        after(pool, s["mid_ready"], b, 1, 1)
                        pool.tensor_tensor(x_res[:, :, :], x_mid_t[:, :, :],
                                           mod[:, 3:4, :].broadcast_to([P, TT, D]), ALU.add).then_inc(s["res_ready"], 1)
                        inverse_std(b, 1)

        @block.tensor
        def _(pe):
            pe.wait_ge(small_loaded, 16 * SMALL_LOADS)
            pe.wait_ge(cond_ready, 1)
            for c in range(4):
                for k in range(DC):
                    mm = pe.matmul(dense_bank[0][:, B * c:B * c + B], w_t[:, k, P * c:P * c + P], cond_g[:, k, :],
                                   start=(k == 0), stop=(k == DC - 1))
            mm.then_inc(tp_ready, 1)
            for c in range(DC):
                for k in range(DC):
                    mm = pe.matmul(dense_bank[1][:, B * c:B * c + B], ada1[:, k, P * c:P * c + P], cond_t[:, k, :],
                                   start=(k == 0), stop=(k == DC - 1))
            mm.then_inc(tp_ready, 1)
            pe.wait_ge(silu_ready, DC)
            for c in range(3):
                bank = (score_bank[0], score_bank[1], turned_bank[0])[c]
                for k in range(DC):
                    mm = pe.matmul(bank[0:B, :], u_t[:, k, :], ada2[:, k, L * c:L * c + L],
                                   start=(k == 0), stop=(k == DC - 1))
                mm.then_inc(ada_ready, 1)
            pe.wait_ge(setup_done, 1)

            for blk, s in enumerate(S):
                pe.wait_ge(w_loaded, W_COUNT[blk])

                def transposes(b, name, src, s=s):
                    for c in range(DC):
                        k = ITEM[name, c]
                        bank_free(pe, s, b, k)
                        for t in range(TT):
                            mm = pe.transpose(dense_bank[k % 2][:, P * t:P * t + P], src[:, t, P * c:P * c + P],
                                              ident[:, :])
                        mm.then_inc(s["dense_ready"], 1)

                def front(b, s=s, blk=blk):
                    if blk == 0:
                        after(pe, s["norm_ready"], b, 2, 1)
                        transposes(b, "t1", x_norm)
                    else:
                        after(pe, s["x_loaded"], b, 16, 16)
                        transposes(b, "t1", x_in_t)
                    for c in range(DC):
                        item_read(pe, s, b, ITEM["t1", c])
                    for c in range(4):
                        k = ITEM["qk", c]
                        bank_free(pe, s, b, k)
                        col = D * (c % 2) + P * (c // 2)
                        for f in range(DC):
                            mm = pe.matmul(dense_bank[k % 2][:, :], w_qkv[:, f, col:col + P], feat[:, f, :],
                                           start=(f == 0), stop=(f == DC - 1))
                        mm.then_inc(s["dense_ready"], 1)
                    for t in range(TT):
                        k = ITEM["v", t]
                        bank_free(pe, s, b, k)
                        for f in range(DC):
                            mm = pe.matmul(dense_bank[k % 2][:, 0:D], feat[:, f, P * t:P * t + P],
                                           w_qkv[:, f, 2 * D:3 * D], start=(f == 0), stop=(f == DC - 1))
                        mm.then_inc(s["dense_ready"], 1)

                def scores(b, u, s=s):
                    g, half, j = u // 8, u // 4 % 2, u % 4
                    if u % 8 == 0:
                        loaded = (s["group0_loaded"], s["group1_loaded"])[g % 2]
                        after(pe, loaded, b, 2 * 9 * 16, (g // 2 + 1) * 9 * 16)
                    for i in range(2):
                        t = 2 * u + i
                        after(pe, s["scores_used"], b, TILES, t + 1)
                        q0 = HALF * half + P * i
                        mm = pe.matmul(score_bank[t % 2][:, :], q_rows[:, g % 2, j, q0:q0 + P],
                                       k_rows[:, g % 2, j, :], start=True, stop=True)
                        mm.then_inc(s["scores_ready"], 1)

                def release_group(b, g, s=s):
                    after(pe, s["scores_ready"], b, TILES, 16 * (g + 1))
                    pe.sem_inc(s["group_used"], 1)

                def turn(b, u, s=s):
                    after(pe, s["shifted_ready"], b, UNITS, u + 1)
                    for pair in range(2):
                        z = 2 * u + pair
                        after(pe, s["probs_ready"], b, TILES, z + 1)
                        for kk in range(2):
                            kt = 2 * pair + kk
                            for i in range(2):
                                mm = pe.transpose(turned_bank[z % 2][:, HALF * kk + P * i:HALF * kk + P * i + P],
                                                  shifted[:, u % 2, i, P * kt:P * kt + P], ident[:, :])
                        mm.then_inc(s["turned_ready"], 1)

                def attend(b, gq, s=s, blk=blk):
                    if gq == 0:
                        for t in range(TT):
                            item_read(pe, s, b, ITEM["v", t])
                        if blk == 1:
                            after(pe, s["vmask_ready"], b, 1, 1)
                    after(pe, s["probs_ready"], b, TILES, 8 * gq + 8 + 2)
                    after(pe, s["head_out_ready"], b, GQ, gq + 1)
                    for kt in range(TT):
                        for j in range(HG):
                            mm = pe.matmul(pv_bank[SLOT * j:SLOT * j + SLOT, 0:HALF],
                                           v_ext[:, kt, HG * (gq // 2) + j, :],
                                           probs[:, (4 * gq + j) % 8, kt, :], start=(kt == 0), stop=(kt == TT - 1),
                                           skip_group_check=True)
                    mm.then_inc(s["probs_used"], 1)

                def spread_sums(b, gq, s=s):
                    after(pe, s["head_out_ready"], b, GQ, gq + 1 + 1)
                    after(pe, s["attn_ready"], b, GQ, gq + 2)
                    pe.matmul(den_bank[:, 0:HALF], den_select[:, :], head_out[:, gq % 2, :], start=True, stop=True)\
                        .then_inc(s["den_ready"], 1)

                def attention(b):
                    for k in range(UNITS + 3):
                        if k < UNITS:
                            scores(b, k)
                        if k >= 10 and (k - 10) % 8 == 0:
                            release_group(b, (k - 10) // 8)
                        if 1 <= k <= UNITS:
                            turn(b, k - 1)
                        if k >= 5 and (k - 5) % 4 == 0:
                            attend(b, (k - 5) // 4)
                        if k >= 6 and (k - 6) % 4 == 0:
                            spread_sums(b, (k - 6) // 4)

                def back(b, s=s):
                    after(pe, s["attn_ready"], b, GQ, GQ + 2)
                    for t in range(TT):
                        k = ITEM["wout", t]
                        bank_free(pe, s, b, k)
                        for g in range(G):
                            mm = pe.matmul(dense_bank[k % 2][:, 0:D], attn[:, g, P * t:P * t + P], w_out[:, g, :],
                                           start=(g == 0), stop=(g == G - 1))
                        mm.then_inc(s["dense_ready"], 1)
                    if blk == 0:
                        after(pe, s["norm_ready"], b, 2, 2)
                        transposes(b, "t2", x_norm)
                    else:
                        after(pe, s["mid_ready"], b, 1, 1)
                        transposes(b, "t2", x_mid_t)
                    for c in range(DC):
                        item_read(pe, s, b, ITEM["t2", c])
                    for c in range(FCH):
                        k = ITEM["up", c]
                        bank_free(pe, s, b, k)
                        for f in range(DC):
                            mm = pe.matmul(dense_bank[k % 2][:, :], w_up[:, f, P * c:P * c + P], feat[:, f, :],
                                           start=(f == 0), stop=(f == DC - 1))
                        mm.then_inc(s["dense_ready"], 1)
                    for c in range(2):
                        item_read(pe, s, b, ITEM["up", FCH - 2 + c])
                    for t in range(TT):
                        k = ITEM["down", t]
                        bank_free(pe, s, b, k)
                        for c in range(FCH):
                            mm = pe.matmul(dense_bank[k % 2][:, 0:D], hidden[:, c, P * t:P * t + P], w_down[:, c, :],
                                           start=(c == 0), stop=(c == FCH - 1))
                        mm.then_inc(s["dense_ready"], 1)

                with pe.Fori(0, B) as b:
                    front(b)
                    attention(b)
                    back(b)

        @block.scalar
        def _(act):
            act.wait_ge(small_loaded, 16 * SMALL_LOADS)
            act.activation(cond_g[:, :, :], cond_t[:, :, :], ACT.Gelu_apprx_tanh).then_inc(cond_ready, 1)
            act.wait_ge(tp_ready, 2)
            for c in range(DC):
                act.activation(u_t[:, c, :], dense_bank[1][:, B * c:B * c + B], ACT.Silu,
                               bias=ada1_col[:, c:c + 1]).then_inc(silu_ready, 1)
            act.wait_ge(setup_done, 1)

            for blk, s in enumerate(S):
                act.wait_ge(w_loaded, W_COUNT[blk])

                def front(b, s=s, blk=blk):
                    for c in range(DC):
                        k = ITEM["t1", c]
                        after(act, s["dense_ready"], b, ND, k + 1)
                        if blk == 0:
                            act.activation(feat[:, c, :], dense_bank[k % 2][:, :], ACT.Identity,
                                           scale=ab[:, 0, c, bass.ds(b, 1)], bias=ab[:, 1, c, bass.ds(b, 1)])\
                                .then_inc(used(s, k), 1)
                        else:
                            act.activation(feat[:, c, :], dense_bank[k % 2][:, :], ACT.Copy).then_inc(used(s, k), 1)
                    after(act, s["base_free"], b, 1, 1)
                    for c in range(4):
                        k = ITEM["qk", c]
                        after(act, s["dense_ready"], b, ND, k + 1)
                        act.activation(qk_high[:, c, :], dense_bank[k % 2][:, :], ACT.Copy,
                                       scale=QUERY_SCALE if c % 2 == 0 else 1.0).then_inc(s["high_ready"], 1)
                    if blk == 1:
                        after(act, s["col_ready"], b, 1, 1)
                    else:
                        after(act, s["probs_used"], b, GQ, 2)
                    for t in range(TT):
                        k = ITEM["v", t]
                        after(act, s["dense_ready"], b, ND, k + 1)
                        src = dense_bank[k % 2][:, 0:D].rearrange("p (h e) -> p h e", h=H)
                        if blk == 0:
                            act.activation(v_ext[:, t, :, 0:HD], src, ACT.Copy).then_inc(used(s, k), 1)
                        else:
                            act.activation(v_ext[:, t, :, 0:HD], src, ACT.Copy, scale=mask_colf[:, t:t + 1])\
                                .then_inc(used(s, k), 1)

                def make_bias(b, u, s=s):
                    g, half, j = u // 8, u // 4 % 2, u % 4
                    h = HG * g + j
                    after(act, s["bias_used"], b, UNITS, u + 1)
                    act.activation(bias[:, u % 2, :, :], dist[:, 2 * half:2 * half + 2, :], ACT.Copy,
                                   scale=neg_scale[:, h:h + 1]).then_inc(s["bias_ready"], 1)

                def exps(b, u, s=s):
                    if u % 4 == 0:
                        after(act, s["probs_used"], b, GQ, u // 4 + 1)
                    for pair in range(2):
                        z = 2 * u + pair
                        after(act, s["turned_ready"], b, TILES, z + 1)
                        act.activation(probs[:, u % 8, 2 * pair:2 * pair + 2, :],
                                       turned_bank[z % 2][:, :].rearrange("p (a c) -> p a c", a=2), ACT.Exp)\
                            .then_inc(s["probs_ready"], 1)

                def take_out(b, gq, s=s):
                    after(act, s["probs_used"], b, GQ, gq + 1 + 2)
                    after(act, s["attn_ready"], b, GQ, gq + 1)
                    act.activation(head_out[:, gq % 2, :], pv_bank[:, 0:HALF], ACT.Copy).then_inc(s["head_out_ready"], 1)

                def attention(b, blk=blk):
                    if blk == 0:
                        make_bias(b, 0)
                        make_bias(b, 1)
                    for u in range(UNITS):
                        exps(b, u)
                        if blk == 0 and u + 2 < UNITS:
                            make_bias(b, u + 2)
                        if u >= 5 and (u - 5) % 4 == 0:
                            take_out(b, (u - 5) // 4)
                    take_out(b, GQ - 1)

                def back(b, s=s, blk=blk):
                    if blk == 1:
                        for t in range(TT):
                            k = ITEM["wout", t]
                            after(act, s["dense_ready"], b, ND, k + 1)
                            act.activation(branch[:, t, :], dense_bank[k % 2][:, 0:D], ACT.Copy)\
                                .then_inc(used(s, k), 1)
                    for c in range(DC):
                        k = ITEM["t2", c]
                        after(act, s["dense_ready"], b, ND, k + 1)
                        if blk == 0:
                            act.activation(feat[:, c, :], dense_bank[k % 2][:, :], ACT.Identity,
                                           scale=ln2_gb[:, 0, c:c + 1], bias=ln2_gb[:, 1, c:c + 1])\
                                .then_inc(used(s, k), 1)
                        else:
                            act.activation(feat[:, c, :], dense_bank[k % 2][:, :], ACT.Copy).then_inc(used(s, k), 1)
                    for c in range(FCH):
                        k = ITEM["up", c]
                        after(act, s["dense_ready"], b, ND, k + 1)
                        act.activation(hidden[:, c, :], dense_bank[k % 2][:, :],
                                       ACT.Gelu_apprx_tanh if blk == 0 else ACT.Gelu, bias=up_bias[:, c:c + 1])\
                            .then_inc(used(s, k), 1)

                with act.Fori(0, B) as b:
                    front(b)
                    attention(b)
                    back(b)

        @block.vector
        def _(dve):
            steps = 0

            def step(ins):
                nonlocal steps
                steps += 1
                ins.then_inc(setup_step, 1)
                dve.wait_ge(setup_step, steps)

            dve.memset(w_out[:, :, :], 0.0).then_inc(dve_consts, 1)
            dve.memset(no_bias[:, :], 0.0).then_inc(dve_consts, 1)
            step(dve.memset(v_ext[:, :, :, :], 0.0))
            dve.memset(v_ext[:, :, :, HD], 1.0).then_inc(dve_consts, 1)
            dve.memset(q_rows[KROWS:KROWS + 1, :, :, :].bitcast(F32), 1.0).then_inc(dve_consts, 1)
            for s in S:
                for name, n in (("base_free", 1), ("group_used", 2), ("scores_used", 2), ("bias_used", 2),
                                ("probs_ready", 2), ("probs_used", 2), ("head_out_ready", 1), ("attn_ready", 2),
                                ("dense_used0", 1), ("dense_used1", 1), ("chain", 1),
                                ("y_stored", 16)):
                    dve.sem_inc(s[name], n)
            dve.wait_ge(small_loaded, 16 * SMALL_LOADS)
            step(dve.tensor_scalar_mul(neg_scale[:, :], neg_scale[:, :], -1.0))
            dve.wait_ge(tp_ready, 1)
            step(dve.tensor_tensor(tp[:, :, :], dense_bank[0][:, 0:4 * B].rearrange("p (c b) -> p c b", c=4),
                                   bt_col[:, :].unsqueeze(2).broadcast_to([P, 4, B]), ALU.add))
            step(dve.tensor_scalar_add(tp[:, 0:2, :], tp[:, 0:2, :], 1.0))
            step(dve.tensor_tensor(ab[:, 0, :, :], tp[:, 0:2, :],
                                   ln1_gb[:, 0, :].unsqueeze(2).broadcast_to([P, DC, B]), ALU.mult))
            step(dve.tensor_tensor(ab[:, 1, :, :], tp[:, 0:2, :],
                                   ln1_gb[:, 1, :].unsqueeze(2).broadcast_to([P, DC, B]), ALU.mult))
            step(dve.tensor_tensor(ab[:, 1, :, :], ab[:, 1, :, :], tp[:, 2:4, :], ALU.add))
            for c in range(3):
                dve.wait_ge(ada_ready, c + 1)
                bank = (score_bank[0], score_bank[1], turned_bank[0])[c]
                step(dve.tensor_tensor(ada[:, L * c:L * c + L], bank[0:B, :], ada2_bias[:, L * c:L * c + L], ALU.add))
            for n in range(2):
                shift, scale, gate = (ada[:, (3 * n + m) * D:(3 * n + m + 1) * D] for m in range(3))
                step(dve.scalar_tensor_tensor(out=mod_out[:, 2 * n * D:(2 * n + 1) * D], in0=scale, scalar=1.0,
                                              in1=gate, op0=ALU.add, op1=ALU.mult))
                step(dve.tensor_tensor(mod_out[:, (2 * n + 1) * D:(2 * n + 2) * D], shift, gate, ALU.mult))
            assert steps == SETUP_STEPS
            dve.wait_ge(setup_done, 1)

            for blk, s in enumerate(S):
                dve.wait_ge(w_loaded, W_COUNT[blk])

                def layer_norm(b, n, src, s=s):
                    for t in range(TT):
                        ins = dve.bn_stats(stats[:, t, :], src[:, t, :])
                    ins.then_inc(s["stats_ready"], 1)
                    after_alone(dve, s["stats_ready"], b, 2, n + 1)
                    for t in range(TT):
                        ins = dve.bn_aggr(mean_var[:, t, :], stats[:, t, :])
                    ins.then_inc(s["mean_ready"], 1)
                    after(dve, s["rstd_ready"], b, 2, n + 1)
                    for t in range(TT):
                        ins = dve.tensor_scalar(x_norm[:, t, :], src[:, t, :], mean_var[:, t, 0:1], rstd[:, t:t + 1],
                                                ALU.subtract, ALU.mult)
                    ins.then_inc(s["norm_ready"], 1)

                def front(b, s=s, blk=blk):
                    if blk == 0:
                        after(dve, s["x_loaded"], b, 16, 16)
                        layer_norm(b, 0, x_in_t)
                    for c in range(4):
                        k = ITEM["qk", c]
                        after(dve, s["high_ready"], b, 4, c + 1)
                        dve.scalar_tensor_tensor(out=qk_low[:, c, :], in0=dense_bank[k % 2][:, :],
                                                 scalar=QUERY_SCALE if c % 2 == 0 else 1.0,
                                                 in1=qk_high[:, c, :].bitcast(F32), op0=ALU.mult,
                                                 op1=ALU.subtract).then_inc(used(s, k), 1)

                def shift_scores(b, u, s=s, blk=blk):
                    if blk == 0:
                        after(dve, s["bias_ready"], b, UNITS, u + 1)
                    if u >= 2:
                        after(dve, s["turned_ready"], b, TILES, 2 * (u - 2) + 2)
                    for i in range(2):
                        t = 2 * u + i
                        after_alone(dve, s["scores_ready"], b, TILES, t + 1)
                        dve.tensor_tensor_reduce(shifted[:, u % 2, i, :], score_bank[t % 2][:, :],
                                                 bias[:, u % 2, i, :] if blk == 0 else no_bias[:, :],
                                                 1.0, -3.0e38, ALU.add, ALU.max, row_max[:, t % 4:t % 4 + 1])\
                            .then_inc(s["scores_used"], 1)
                    for i in range(2):
                        t = 2 * u + i
                        after(dve, s["scores_used"], b, TILES, t + 1 + 2)
                        ins = dve.tensor_scalar(shifted[:, u % 2, i, :], shifted[:, u % 2, i, :],
                                                row_max[:, t % 4:t % 4 + 1], None, ALU.subtract)
                        ins.then_inc(s["bias_used"] if i == 0 else s["shifted_ready"], 1)

                def divide(b, gq, s=s):
                    if gq == 0:
                        after(dve, s["dense_ready"], b, ND, ITEM["v", 0])
                    after(dve, s["den_ready"], b, GQ, gq + 1)
                    q0 = HALF * (gq % 2)
                    dve.reciprocal(inv_sum[:, :], den_bank[:, 0:HALF]).then_inc(s["inv_ready"], 1)
                    after(dve, s["inv_ready"], b, GQ, gq + 1)
                    dve.tensor_tensor(attn[:, gq // 2, q0:q0 + HALF], head_out[:, gq % 2, :], inv_sum[:, :],
                                      ALU.mult).then_inc(s["attn_ready"], 1)

                def attention(b):
                    for u in range(UNITS):
                        shift_scores(b, u)
                        if u >= 6 and (u - 6) % 4 == 0:
                            divide(b, (u - 6) // 4)
                    divide(b, GQ - 1)

                def back0(b, s=s):
                    after(dve, s["res_loaded"], b, 16, 16)
                    for t in range(TT):
                        k = ITEM["wout", t]
                        after(dve, s["dense_ready"], b, ND, k + 1)
                        dve.tensor_tensor(x_mid_t[:, t, :], x_res[:, t, :], dense_bank[k % 2][:, 0:D], ALU.add)\
                            .then_inc(used(s, k), 1)
                    for t in range(2):
                        item_read(dve, s, b, ITEM["wout", 2 + t])
                    layer_norm(b, 1, x_mid_t)
                    dve.sem_inc(s["mid_ready"], 1)
                    after(dve, s["res_ready"], b, 1, 1)
                    after(dve, s["y_stored"], b, 16, 16)
                    for t in range(TT):
                        k = ITEM["down", t]
                        after(dve, s["dense_ready"], b, ND, k + 1)
                        dve.tensor_tensor(y_t[:, t, :], x_mid_t[:, t, :], dense_bank[k % 2][:, 0:D], ALU.add)\
                            .then_inc(used(s, k), 1)
                    for t in range(2):
                        item_read(dve, s, b, ITEM["down", 2 + t])
                    dve.sem_inc(s["y_ready"], 1)

                def modulate(b, n, out_t, done, s=s):
                    after(dve, s["norm_ready"], b, 2, n + 1)
                    dve.tensor_tensor(x_norm[:, :, :], x_norm[:, :, :],
                                      mod[:, 2 * n:2 * n + 1, :].broadcast_to([P, TT, D]), ALU.mult)\
                        .then_inc(s["chain"], 1)
                    after(dve, s["chain"], b, 4, 2 * n + 1 + 1)
                    after(dve, s["res_ready"], b, 2, n + 1)
                    dve.tensor_tensor(out_t, x_norm[:, :, :], x_res[:, :, :], ALU.add).then_inc(done, 1)
                    after(dve, done, b, 1, 1)
                    dve.sem_inc(s["chain"], 1)

                def back1(b, s=s):
                    for t in range(2):
                        item_read(dve, s, b, ITEM["wout", 2 + t])
                    layer_norm(b, 0, branch)
                    modulate(b, 0, x_mid_t[:, :, :], s["mid_ready"])
                    for t in range(TT):
                        k = ITEM["down", t]
                        after(dve, s["dense_ready"], b, ND, k + 1)
                        dve.tensor_tensor(branch[:, t, :], down_bias[:, :], dense_bank[k % 2][:, 0:D], ALU.add)\
                            .then_inc(used(s, k), 1)
                    for t in range(2):
                        item_read(dve, s, b, ITEM["down", 2 + t])
                    layer_norm(b, 1, branch)
                    after(dve, s["y_stored"], b, 16, 16)
                    modulate(b, 1, y_t[:, :, :], s["y_ready"])

                with dve.Fori(0, B) as b:
                    front(b)
                    attention(b)
                    (back0, back1)[blk](b)


SMALL_LOADS = 14
POOL_CONSTS = 5
DVE_CONSTS = 4
SETUP_STEPS = 2 + 5 + 3 + 4

_INS = ['x', 'cond_1024', 'mask_BxS_bf1', 'mask_BxS_bk0', 'L0_cond_torus_dist', 'L0_cond_ln1_g', 'L0_cond_ln1_b',
        'L0_cond_Wqkv', 'L0_cond_Wout', 'L0_cond_torus_scale', 'L0_cond_ln2_g', 'L0_cond_ln2_b', 'L0_cond_W1',
        'L0_cond_b1', 'L0_cond_W2', 'L0_cond_b2', 'L0_cond_Wt', 'L0_cond_bt', 'L1_cond_qkv_w', 'L1_cond_proj_w',
        'L1_cond_proj_b', 'L1_cond_fc1_w', 'L1_cond_fc1_b', 'L1_cond_fc2_w', 'L1_cond_fc2_b', 'L1_cond_ada1_w',
        'L1_cond_ada1_b', 'L1_cond_ada2_w', 'L1_cond_ada2_b']


def kernel(**inputs):
    import numpy as np
    import concourse.bacc as bacc
    from concourse.bass_utils import run_bass_kernel_spmd

    nc = bacc.Bacc("TRN2", target_bir_lowering=False, num_devices=1)
    arrays, d = {}, {}
    for name in _INS:
        a = np.ascontiguousarray(inputs[name])
        arrays[f"in_{name}"] = a
        d[name] = nc.dram_tensor(f"in_{name}", a.shape, mybir.dt.from_np(a.dtype), kind="ExternalInput").ap()
    out = nc.dram_tensor("out", inputs["x"].shape, F32, kind="ExternalOutput").ap()
    build(nc, d, out)
    r = run_bass_kernel_spmd(nc, [arrays], core_ids=[0])
    return r.results[0]["out"]
```

```python
from contextlib import ExitStack

import concourse.bass as bass
from concourse import mybir

ALU = mybir.AluOpType
ACT = mybir.ActivationFunctionType
F32 = mybir.dt.float32
F32R = mybir.dt.float32r
U8 = mybir.dt.uint8

P = 128
EPS = 1e-5
PAD = 1e30
QUERY_SCALE = 0.25


def build(nc, d, out):
    B, L, D = d["x"].shape
    H = d["L0_cond_torus_scale"].shape[0]
    F = d["L0_cond_W1"].shape[1]
    HD = D // H
    TT = L // P
    DC = D // P
    FCH = F // P
    HG = 4
    G = H // HG
    SLOT = P // HG
    KROWS = 4 * HD
    UNITS = 2 * H
    HALF = L // 2
    GQ = 2 * G
    TILES = 2 * UNITS
    RING = 6
    assert HD == 16 and TT == 4 and DC == 2 and G == 4 and FCH == 8

    AT_STEP = {0: [("v", 0)], 1: [("v", 1)], 2: [("v", 2)], 3: [("v", 3)], 4: [("t3", 0)], 5: [("t3", 1)],
               6: [("t1", 0)], 7: [("t1", 1)], 8: [("wout", 0)], 9: [("wout", 1)], 10: [("wout", 2)],
               11: [("wout", 3)], 12: [("qk", 0)], 13: [("qk", 1)], 14: [("qk", 2)], 15: [("qk", 3)],
               17: [("t2", 0)], 18: [("t2", 1)], 21: [("up", 0), ("up", 1)], 23: [("up", 2), ("up", 3)],
               25: [("up", 4), ("up", 5)], 27: [("up", 6), ("up", 7)], 29: [("down", 0)], 30: [("down", 1)],
               31: [("down", 2)], 32: [("down", 3)]}
    NORM_STEP = [{2: ("stats", 0), 4: ("norm", 0), 13: ("stats", 1), 15: ("norm", 1)},
                 {13: ("stats", 0), 15: ("norm", 0), 33: ("stats", 1), 34: ("norm", 1)}]
    FRONT = ("t1", "qk")
    BACK = ("t3", "wout", "t2", "up", "down")
    ORDER = [p for k in range(UNITS + 3) for p in AT_STEP.get(k, [])]
    ND = len(ORDER)
    assert ND % 2 == 0

    def kind(piece):
        return -1 if piece[0] in BACK else 1 if piece[0] in FRONT else 0

    PASSED = [(p, 0) for p in ORDER if kind(p) == 1]
    for turn in range(B):
        PASSED += [(p, turn + kind(p)) for p in ORDER if 0 <= turn + kind(p) < B]
    PASSED += [(p, B - 1) for p in ORDER if kind(p) == -1]
    PLACE = {x: n for n, x in enumerate(PASSED)}

    def place(piece, b):
        if isinstance(b, int):
            return PLACE[piece, b]
        return PLACE[piece, 2] - 2 * ND + b * ND

    for p in ORDER:
        for turn in range(1, B - 1):
            assert PLACE[p, turn + kind(p)] == PLACE[p, 2] + (turn + kind(p) - 2) * ND, p
        assert len({PLACE[p, b] % 2 for b in range(B)}) == 1

    def bank_of(piece):
        return PLACE[piece, 2] % 2

    with ExitStack() as ctx:
        def sb(name, shape, dt=F32):
            return ctx.enter_context(nc.sbuf_tensor(name, shape, dt))

        def sem(name):
            return ctx.enter_context(nc.semaphore(name))

        def dram(name, shape):
            return nc.dram_tensor(name, shape, F32, kind="Internal").ap()

        x_mid = dram("x_mid", (B, L, D))
        qk_halves = dram("qk_halves", (2, B, 2, 2, D, L))
        mod_rows = dram("mod_rows", (B, 4 * D))

        score_bank = [ctx.enter_context(nc.psum_tensor(f"score{i}", [P, L], F32)) for i in range(2)]
        turned_bank = [ctx.enter_context(nc.psum_tensor(f"turned{i}", [P, L], F32)) for i in range(2)]
        pv_bank = ctx.enter_context(nc.psum_tensor("pv", [P, L], F32))
        token_bank = ctx.enter_context(nc.psum_tensor("token", [P, L], F32))
        dense_bank = [ctx.enter_context(nc.psum_tensor(f"dense{i}", [P, L], F32)) for i in range(2)]

        w_qkv = sb("w_qkv", [P, 2, DC, 3 * D], F32R)
        w_out = sb("w_out", [P, 2, DC, D], F32R)
        w_up = sb("w_up", [P, 2, DC, F], F32R)
        w_down = sb("w_down", [P, FCH, D])
        up_bias = sb("up_bias", [P, FCH])
        down_bias = sb("down_bias", [P, D])
        out_bias = sb("out_bias", [P, D])
        ident = sb("ident", [P, P])
        minus_half = sb("minus_half", [P, TT])
        neg_scale = sb("neg_scale", [P, H])
        dist = sb("dist", [P, TT, L])
        no_bias = sb("no_bias", [P, L])
        ln2_gb = sb("ln2_gb", [P, 2, DC])
        ab = sb("ab", [P, 2, DC, B])
        x_in_t = sb("x_in_t", [P, TT, D])
        x_res = sb("x_res", [P, TT, D])
        x_norm = sb("x_norm", [P, TT, D])
        branch = dist[:, 0:2, :].rearrange("p a (c n) -> p (a c) n", n=D)
        mod = dist[:, 2:4, :].rearrange("p a (c n) -> p (a c) n", n=D)
        feat_tmp = sb("feat_tmp", [P, DC, L])
        feat_a = sb("feat_a", [P, 2, DC, L], F32R)
        feat_m = sb("feat_m", [P, 2, DC, L], F32R)
        qk_high = sb("qk_high", [P, 4, L], F32R)
        qk_low = sb("qk_low", [P, 4, L], F32R)
        q_rows = sb("q_rows", [KROWS + 1, 2, HG, L], F32R)
        k_rows = sb("k_rows", [KROWS + 1, 2, HG, L], F32R)
        v_ext = sb("v_ext", [P, TT, H, SLOT])
        bias = sb("bias", [P, 2, 2, L])
        shifted = sb("shifted", [P, 2, 2, L])
        probs = sb("probs", [P, RING, TT, HALF])
        head_out = sb("head_out", [P, 2, HALF])
        inv_sum = sb("inv_sum", [P, 2, HG])
        attn = sb("attn", [P, TT, D])
        hidden = sb("hidden", [P, FCH, L])
        row_max = sb("row_max", [P, 4])
        stats = sb("stats", [P, 2, TT, 6])
        mean_var = sb("mean_var", [P, 2, TT, 2])
        var_eps = sb("var_eps", [P, 2, TT])
        rstd = sb("rstd", [P, 2, TT])
        mask_row = sb("mask_row", [KROWS + 1, L], U8)
        mask_neg = sb("mask_neg", [KROWS + 1, L], F32R)
        mask_col = sb("mask_col", [P, TT], U8)
        mask_colf = sb("mask_colf", [P, TT])
        cond_t = sb("cond_t", [P, DC, B])
        cond_g = sb("cond_g", [P, DC, B])
        u_t = sb("u_t", [P, DC, B])
        tp = sb("tp", [P, 4, B])
        bt_col = sb("bt_col", [P, 4])
        ada1_col = sb("ada1_col", [P, DC])
        ln1_gb = sb("ln1_gb", [P, 2, DC])
        raw = hidden[:, :, :].rearrange("p a b -> p (a b)")
        ada2 = raw[:, 0:3072].rearrange("p (c n) -> p c n", c=DC)
        w_t = raw[:, 3072:4096].rearrange("p (c n) -> p c n", c=DC)
        ada1 = x_in_t[:, 0:2, :]
        early = shifted[0:B, :, :, :].rearrange("p a b c -> p (a b c)")
        ada2_bias = early[:, 0:1536]
        ada = bias[0:B, :, :, :].rearrange("p a b c -> p (a b c)")[:, 0:1536]
        mod_out = x_res[0:B, :, :].rearrange("p a b -> p (a b)")
        staged = probs[:, :, :, :].rearrange("p a b c -> p (a b c)")
        raw_qkv = staged[:, 0:1536].rearrange("p (c n) -> p c n", c=DC)
        raw_out = staged[:, 1536:2048].rearrange("p (c n) -> p c n", c=DC)
        raw_up = staged[:, 2048:4096].rearrange("p (c n) -> p c n", c=DC)

        small_loaded = sem("small_loaded")
        w_loaded = [sem("w_loaded0"), sem("w_loaded1")]
        w_high = [sem("w_high0"), sem("w_high1")]
        w_split = [sem("w_split0"), sem("w_split1")]
        pool_consts = sem("pool_consts")
        dve_consts = sem("dve_consts")
        cond_ready = sem("cond_ready")
        tp_ready = sem("tp_ready")
        silu_ready = sem("silu_ready")
        ada_ready = sem("ada_ready")
        setup_step = sem("setup_step")
        mod_stored = sem("mod_stored")
        setup_done = sem("setup_done")
        carried = sem("carried")
        S = []
        for blk in range(2):
            n = {}
            for name in ("x_loaded", "res_loaded", "mask_loaded", "mask_ready", "col_loaded", "col_ready",
                         "vmask_ready", "mod_loaded", "halves_stored0", "halves_stored1", "base_free",
                         "group0_loaded", "group1_loaded", "group_used", "scores_ready", "scores_used",
                         "bias_ready", "bias_used", "shifted_ready", "turned_ready", "probs_ready", "probs_used",
                         "head_out_ready", "token_ready", "inv_ready", "attn_ready", "dense_ready",
                         "dense_used0", "dense_used1", "t1_high", "t2_high", "t3_high", "qk_high", "t1_low", "t2_low",
                         "stats_ready0", "stats_ready1",
                         "mean_ready0", "mean_ready1", "var_ready0", "var_ready1", "rstd_ready0", "rstd_ready1",
                         "norm_ready0", "norm_ready1", "mid_ready", "res_ready0", "res_ready1", "scaled",
                         "y_ready", "y_stored"):
                n[name] = sem(f"b{blk}_{name}")
            S.append(n)

        def after(eng, s, b, per_batch, n):
            eng.wait_ge(s, b * per_batch + n)

        def after_alone(eng, s, b, per_batch, n):
            eng.wait_ge(s, b * per_batch + n)
            eng.sem_inc(carried, 1)

        def used(s, piece):
            return (s["dense_used0"], s["dense_used1"])[bank_of(piece)]

        def count_in_bank(piece, b):
            if isinstance(b, int):
                return PLACE[piece, b] // 2
            return PLACE[piece, 2] // 2 - ND + b * (ND // 2)

        def bank_free(eng, s, piece, b):
            eng.wait_ge(used(s, piece), count_in_bank(piece, b) + 1)

        def piece_read(eng, s, piece, b):
            eng.wait_ge(used(s, piece), count_in_bank(piece, b) + 2)

        def halves_ready(eng, s, blk, name, b):
            if blk == 0 and name != "t3":
                after(eng, s[name + "_low"], b, DC, DC)
            else:
                for c in range(DC):
                    piece_read(eng, s, (name, c), b)

        def piece_ready(eng, s, piece, b):
            eng.wait_ge(s["dense_ready"], place(piece, b) + 1)

        def run(eng, prologue, turn, epilogue):
            prologue()
            turn(0, False, True)
            with eng.Fori(1, B - 1) as b:
                turn(b, True, True)
            turn(B - 1, True, False)
            epilogue()

        def pieces(k, b, has_back, has_front):
            for p in AT_STEP.get(k, []):
                if {-1: has_back, 0: True, 1: has_front}[kind(p)]:
                    yield p, b + kind(p)

        block = ctx.enter_context(nc.Block())
        W_LOADS = [0, 0]

        @block.sync
        def _(sp):
            def load_small(dst, src):
                sp.dma_start(dst, src).then_inc(small_loaded, 16)

            def load_weights(blk, pre, qkv, wout, up, up_b, down, down_b):
                for dst, src in ((raw_qkv, d[pre + qkv].rearrange("(c p) n -> p c n", p=P)),
                                 (raw_out, d[pre + wout].rearrange("(c p) n -> p c n", p=P)),
                                 (raw_up, d[pre + up].rearrange("(c p) n -> p c n", p=P)),
                                 (w_down[:, :, :], d[pre + down].rearrange("(c p) n -> p c n", p=P)),
                                 (up_bias[:, :], d[pre + up_b].rearrange("(c p) -> p c", p=P)),
                                 (down_bias[:, :], d[pre + down_b].unsqueeze(0).broadcast_to([P, D])),
                                 (out_bias[:, :], d["L1_cond_proj_b"].unsqueeze(0).broadcast_to([P, D]))):
                    sp.dma_start(dst, src).then_inc(w_loaded[blk], 16)
                    W_LOADS[blk] += 1

            with nc.allow_non_contiguous_dma(reason="small vectors laid on partitions"):
                load_small(cond_t[:, 0, :], d["cond_1024"][:, 0:P].rearrange("b p -> p b"))
                load_small(cond_t[:, 1, :], d["cond_1024"][:, P:D].rearrange("b p -> p b"))
                load_small(w_t, d["L0_cond_Wt"].rearrange("(c p) n -> p c n", p=P))
                load_small(bt_col[:, :], d["L0_cond_bt"].rearrange("(c p) -> p c", p=P))
                load_small(ln1_gb[:, 0, :], d["L0_cond_ln1_g"].rearrange("(c p) -> p c", p=P))
                load_small(ln1_gb[:, 1, :], d["L0_cond_ln1_b"].rearrange("(c p) -> p c", p=P))
                load_small(ln2_gb[:, 0, :], d["L0_cond_ln2_g"].rearrange("(c p) -> p c", p=P))
                load_small(ln2_gb[:, 1, :], d["L0_cond_ln2_b"].rearrange("(c p) -> p c", p=P))
                load_small(ada1, d["L1_cond_ada1_w"].rearrange("(c p) n -> p c n", p=P))
                load_small(ada1_col[:, :], d["L1_cond_ada1_b"].rearrange("(c p) -> p c", p=P))
                load_small(ada2, d["L1_cond_ada2_w"].rearrange("(c p) n -> p c n", p=P))
                load_small(ada2_bias, d["L1_cond_ada2_b"].unsqueeze(0).broadcast_to([B, 6 * D]))
                load_small(neg_scale[:, :], d["L0_cond_torus_scale"].unsqueeze(0).broadcast_to([P, H]))
                load_small(dist[:, :, :], d["L0_cond_torus_dist"][0].rearrange("(t p) k -> p t k", p=P))
                load_weights(0, "L0_cond_", "Wqkv", "Wout", "W1", "b1", "W2", "b2")
                sp.wait_ge(dve_consts, DVE_CONSTS)
                sp.wait_ge(pool_consts, POOL_CONSTS)
                sp.wait_ge(setup_step, SETUP_STEPS)
                sp.dma_start(mod_rows, mod_out).then_inc(mod_stored, 16)
                sp.wait_ge(mod_stored, 16)
                sp.sem_inc(setup_done, 1)

                for blk, s in enumerate(S):
                    x_src = (d["x"], x_mid)[blk]
                    y_dst = (x_mid, out)[blk]
                    mask = (d["mask_BxS_bf1"], d["mask_BxS_bk0"])[blk]

                    def load_x(b, s=s, x_src=x_src):
                        sp.dma_start(x_in_t[:, :, :], x_src[b].rearrange("(t p) n -> p t n", p=P))\
                            .then_inc(s["x_loaded"], 16)

                    def load_res(b, s=s, x_src=x_src):
                        sp.dma_start(x_res[:, :, :], x_src[b].rearrange("(t p) n -> p t n", p=P))\
                            .then_inc(s["res_loaded"], 16)

                    def load_mod(b, s=s):
                        sp.dma_start(mod.rearrange("p a n -> p (a n)"),
                                     mod_rows[b].unsqueeze(0).broadcast_to([P, 4 * D])).then_inc(s["mod_loaded"], 16)

                    def load_mask(b, s=s, mask=mask, blk=blk):
                        sp.dma_start(mask_row[KROWS:KROWS + 1, :], mask[bass.ds(b, 1), :])\
                            .then_inc(s["mask_loaded"], 16)
                        if blk == 1:
                            sp.dma_start(mask_col[:, :], mask[b].rearrange("(t p) -> p t", p=P))\
                                .then_inc(s["col_loaded"], 16)

                    def store_halves(b, s=s, blk=blk):
                        for c in range(4):
                            piece_read(sp, s, ("qk", c), b)
                            sp.sem_inc(carried, 1)
                            rows = slice(P * (c // 2), P * (c // 2) + P)
                            stored = (s["halves_stored0"], s["halves_stored1"])[c // 2]
                            sp.dma_start(qk_halves[blk, b, 0, c % 2, rows, :], qk_high[:, c, :].bitcast(F32))\
                                .then_inc(stored, 16)
                            sp.dma_start(qk_halves[blk, b, 1, c % 2, rows, :], qk_low[:, c, :].bitcast(F32))\
                                .then_inc(stored, 16)

                    def load_group(b, g, s=s, blk=blk):
                        after_alone(sp, (s["halves_stored0"], s["halves_stored1"])[g // 2], b, 64, 64)
                        if g == 2:
                            sp.sem_inc(s["base_free"], 1)
                        after_alone(sp, s["mask_ready"], b, 1, 1)
                        after_alone(sp, s["group_used"], b, G, g + 1)
                        loaded = (s["group0_loaded"], s["group1_loaded"])[g % 2]
                        rows = slice(HG * HD * g, HG * HD * (g + 1))
                        for r in range(4):
                            sp.dma_start(q_rows[HD * r:HD * r + HD, g % 2, :, :].bitcast(F32),
                                         qk_halves[blk, b, r // 2, 0, rows, :]
                                         .rearrange("(h e) n -> e h n", e=HD)).then_inc(loaded, 16)
                            sp.dma_start(k_rows[HD * r:HD * r + HD, g % 2, :, :].bitcast(F32),
                                         qk_halves[blk, b, r % 2, 1, rows, :]
                                         .rearrange("(h e) n -> e h n", e=HD)).then_inc(loaded, 16)
                        sp.dma_start(k_rows[KROWS:KROWS + 1, g % 2, :, :].bitcast(F32),
                                     mask_neg[KROWS:KROWS + 1, :].bitcast(F32).unsqueeze(1)
                                     .broadcast_to([1, HG, L])).then_inc(loaded, 16)

                    def store_y(b, s=s, y_dst=y_dst):
                        after_alone(sp, s["y_ready"], b, 1, 2)
                        sp.dma_start(y_dst[b].rearrange("(t p) n -> p t n", p=P), x_norm[:, :, :])\
                            .then_inc(s["y_stored"], 16)

                    def prologue(s=s, blk=blk):
                        load_x(0)
                        load_mask(0)
                        store_halves(0)
                        load_group(0, 0)
                        load_group(0, 1)

                    def turn(b, has_back, has_front, s=s, blk=blk):
                        if has_back:
                            after_alone(sp, s["y_ready"], b, 1, 0)
                            load_res(b - 1)
                            if blk == 1:
                                load_mod(b - 1)
                        if has_front:
                            if blk == 0:
                                after_alone(sp, s["norm_ready0"], b, 1, 1)
                            load_x(b + 1)
                        load_group(b, 2)
                        load_group(b, 3)
                        if has_front:
                            after_alone(sp, s["group1_loaded"], b, 2 * 9 * 16, 2 * 9 * 16)
                            after_alone(sp, s["group0_loaded"], b, 2 * 9 * 16, 2 * 9 * 16)
                            if blk == 1:
                                after_alone(sp, s["vmask_ready"], b, 1, 1)
                            load_mask(b + 1)
                            store_halves(b + 1)
                            load_group(b + 1, 0)
                        if has_back:
                            store_y(b - 1)
                        if has_front:
                            load_group(b + 1, 1)

                    def epilogue(s=s, blk=blk):
                        sp.wait_ge(s["y_ready"], B)
                        load_res(B - 1)
                        if blk == 1:
                            load_mod(B - 1)
                        store_y(B - 1)
                        sp.wait_ge(s["y_stored"], 16 * (B + 1))

                    if blk == 1:
                        load_weights(1, "L1_cond_", "qkv_w", "proj_w", "fc1_w", "fc1_b", "fc2_w", "fc2_b")
                    run(sp, prologue, turn, epilogue)

        @block.gpsimd
        def _(pool):
            pool.memset(ident[:, :], 0.0).then_inc(pool_consts, 1)
            pool.memset(minus_half[:, :], -0.5).then_inc(pool_consts, 1)
            pool.wait_ge(pool_consts, 1)
            pool.affine_select(out=ident[:, :], in_=ident[:, :], compare_op=ALU.not_equal, fill=1.0, base=0,
                               pattern=[[-1, P]], channel_multiplier=1).then_inc(pool_consts, 1)
            pool.wait_ge(setup_done, 1)

            for blk, s in enumerate(S):
                def inverse_std(b, n, s=s):
                    after_alone(pool, s[f"mean_ready{n}"], b, 1, 1)
                    pool.tensor_scalar_add(var_eps[:, n, :], mean_var[:, n, :, 1], EPS).then_inc(s[f"var_ready{n}"], 1)
                    after(pool, s[f"var_ready{n}"], b, 1, 1)
                    pool.tensor_tensor(rstd[:, n, :], var_eps[:, n, :], minus_half[:, :], ALU.pow)\
                        .then_inc(s[f"rstd_ready{n}"], 1)
                    after_alone(pool, s[f"rstd_ready{n}"], b, 1, 1)

                def mask(b, s=s, blk=blk):
                    after_alone(pool, s["mask_loaded"], b, 16, 16)
                    pool.tensor_scalar(mask_neg[KROWS:KROWS + 1, :], mask_row[KROWS:KROWS + 1, :], PAD, -PAD,
                                       ALU.mult, ALU.add).then_inc(s["mask_ready"], 1)
                    after_alone(pool, s["mask_ready"], b, 1, 1)

                def value_mask(b, s=s):
                    after_alone(pool, s["probs_used"], b, GQ, 1)
                    after_alone(pool, s["col_loaded"], b, 16, 16)
                    pool.tensor_copy(mask_colf[:, :], mask_col[:, :]).then_inc(s["col_ready"], 1)
                    after_alone(pool, s["col_ready"], b, 1, 1)
                    pool.tensor_copy(v_ext[:, :, :, HD], mask_colf[:, :].unsqueeze(2).broadcast_to([P, TT, H]))\
                        .then_inc(s["vmask_ready"], 1)

                def add_bias(b, s=s):
                    after(pool, s["norm_ready1"], b, 1, 1)
                    pool.tensor_tensor(x_res[:, :, :], x_res[:, :, :],
                                       down_bias[:, :].unsqueeze(1).broadcast_to([P, TT, D]), ALU.add)\
                        .then_inc(s["res_ready1"], 1)
                    after_alone(pool, s["res_ready1"], b, 1, 1)

                def add_shift(b, n, s=s):
                    if n == 0:
                        after(pool, s["res_loaded"], b, 16, 16)
                        after(pool, s["mod_loaded"], b, 16, 16)
                    else:
                        piece_ready(pool, s, ("t2", DC - 1), b)
                    pool.tensor_tensor(x_res[:, :, :], x_res[:, :, :],
                                       mod[:, 2 * n + 1:2 * n + 2, :].broadcast_to([P, TT, D]), ALU.add)\
                        .then_inc(s[f"res_ready{n}"], 1)
                    after_alone(pool, s[f"res_ready{n}"], b, 1, 1)

                def back(b, blk=blk):
                    if blk == 0:
                        inverse_std(b, 1)
                        add_bias(b)
                    else:
                        add_shift(b, 0)
                        inverse_std(b, 0)
                        add_shift(b, 1)
                        inverse_std(b, 1)

                def prologue(blk=blk):
                    mask(0)
                    if blk == 0:
                        inverse_std(0, 0)

                def turn(b, has_back, has_front, blk=blk):
                    if blk == 1:
                        value_mask(b)
                    if has_front and blk == 0:
                        inverse_std(b + 1, 0)
                    if has_back:
                        back(b - 1)
                    if has_front:
                        mask(b + 1)

                run(pool, prologue, turn, lambda: back(B - 1))

        @block.tensor
        def _(pe):
            pe.wait_ge(small_loaded, 16 * SMALL_LOADS)
            pe.wait_ge(cond_ready, 1)
            for c in range(4):
                for k in range(DC):
                    mm = pe.matmul(dense_bank[0][:, B * c:B * c + B], w_t[:, k, P * c:P * c + P], cond_g[:, k, :],
                                   start=(k == 0), stop=(k == DC - 1))
            mm.then_inc(tp_ready, 1)
            for c in range(DC):
                for k in range(DC):
                    mm = pe.matmul(dense_bank[1][:, B * c:B * c + B], ada1[:, k, P * c:P * c + P], cond_t[:, k, :],
                                   start=(k == 0), stop=(k == DC - 1))
            mm.then_inc(tp_ready, 1)
            pe.wait_ge(silu_ready, DC)
            for c in range(3):
                bank = (score_bank[0], score_bank[1], turned_bank[0])[c]
                for k in range(DC):
                    mm = pe.matmul(bank[0:B, :], u_t[:, k, :], ada2[:, k, L * c:L * c + L],
                                   start=(k == 0), stop=(k == DC - 1))
                mm.then_inc(ada_ready, 1)
            pe.wait_ge(setup_done, 1)

            def products(out_ap, pairs):
                terms = [(left[x], right[y]) for left, right in pairs for x, y in ((0, 0), (0, 1), (1, 0))]
                for n, (left, right) in enumerate(terms):
                    mm = pe.matmul(out_ap, left, right, start=(n == 0), stop=(n == len(terms) - 1))
                return mm

            for blk, s in enumerate(S):
                pe.wait_ge(w_split[blk], 3)

                def halves(t, c, cols):
                    return [t[:, x, c, cols] for x in range(2)]

                def transposes(bank, src, c):
                    for t in range(TT):
                        mm = pe.transpose(bank[:, P * t:P * t + P], src[:, t, P * c:P * c + P], ident[:, :])
                    return mm

                def dense(piece, b, s=s, blk=blk):
                    name, i = piece
                    bank = dense_bank[bank_of(piece)]
                    tokens = slice(P * i, P * i + P)
                    every = slice(0, L)
                    if name == "t1":
                        if blk == 0:
                            after(pe, s["norm_ready0"], b, 1, 1)
                        else:
                            after(pe, s["x_loaded"], b, 16, 16)
                    elif name == "qk" and i == 0:
                        halves_ready(pe, s, blk, "t1", b)
                    elif name == "t3":
                        after(pe, s["attn_ready"], b, GQ, GQ + 2)
                    elif name == "wout" and i == 0:
                        halves_ready(pe, s, blk, "t3", b)
                    elif name == "t2":
                        after(pe, s["norm_ready1" if blk == 0 else "mid_ready"], b, 1, 1)
                    elif name == "up" and i == 0:
                        halves_ready(pe, s, blk, "t2", b)
                    elif name == "down" and i == 0:
                        for c in range(2):
                            piece_read(pe, s, ("up", FCH - 2 + c), b)
                    bank_free(pe, s, piece, b)
                    if name == "t1":
                        mm = transposes(bank, x_norm if blk == 0 else x_in_t, i)
                    elif name == "qk":
                        col = D * (i % 2) + P * (i // 2)
                        mm = products(bank[:, :], [(halves(w_qkv, c, slice(col, col + P)), halves(feat_a, c, every))
                                                   for c in range(DC)])
                    elif name == "v":
                        mm = products(bank[:, 0:D], [(halves(feat_a, c, tokens),
                                                      halves(w_qkv, c, slice(2 * D, 3 * D))) for c in range(DC)])
                    elif name == "t3":
                        mm = transposes(bank, attn, i)
                    elif name == "wout":
                        mm = products(bank[:, 0:D], [(halves(feat_m, c, tokens), halves(w_out, c, slice(0, D)))
                                                     for c in range(DC)])
                    elif name == "t2":
                        mm = transposes(bank, x_norm if blk == 0 else x_res, i)
                    elif name == "up":
                        mm = products(bank[:, :], [(halves(w_up, c, tokens), halves(feat_m, c, every))
                                                   for c in range(DC)])
                    else:
                        for c in range(FCH):
                            mm = pe.matmul(bank[:, 0:D], hidden[:, c, tokens], w_down[:, c, :],
                                           start=(c == 0), stop=(c == FCH - 1))
                    mm.then_inc(s["dense_ready"], 1)

                def scores(b, u, s=s):
                    g, half, j = u // 8, u // 4 % 2, u % 4
                    if u % 8 == 0:
                        loaded = (s["group0_loaded"], s["group1_loaded"])[g % 2]
                        after(pe, loaded, b, 2 * 9 * 16, (g // 2 + 1) * 9 * 16)
                    for i in range(2):
                        t = 2 * u + i
                        after(pe, s["scores_used"], b, TILES, t + 1)
                        q0 = HALF * half + P * i
                        pe.matmul(score_bank[t % 2][:, :], q_rows[:, g % 2, j, q0:q0 + P],
                                  k_rows[:, g % 2, j, :], start=True, stop=True).then_inc(s["scores_ready"], 1)

                def release_group(b, g, s=s):
                    after(pe, s["scores_ready"], b, TILES, 16 * (g + 1))
                    pe.sem_inc(s["group_used"], 1)

                def turn_unit(b, u, s=s):
                    after(pe, s["shifted_ready"], b, UNITS, u + 1)
                    for pair in range(2):
                        z = 2 * u + pair
                        after(pe, s["probs_ready"], b, TILES, z + 1)
                        for kk in range(2):
                            kt = 2 * pair + kk
                            for i in range(2):
                                mm = pe.transpose(turned_bank[z % 2][:, HALF * kk + P * i:HALF * kk + P * i + P],
                                                  shifted[:, u % 2, i, P * kt:P * kt + P], ident[:, :])
                        mm.then_inc(s["turned_ready"], 1)

                def attend(b, gq, s=s, blk=blk):
                    if gq == 0:
                        for t in range(2):
                            piece_read(pe, s, ("v", TT - 2 + t), b)
                        if blk == 1:
                            after(pe, s["vmask_ready"], b, 1, 1)
                    after(pe, s["probs_ready"], b, TILES, 8 * gq + 8 + 2)
                    after(pe, s["head_out_ready"], b, GQ, gq + 1)
                    for kt in range(TT):
                        for j in range(HG):
                            mm = pe.matmul(pv_bank[SLOT * j:SLOT * j + SLOT, 0:HALF],
                                           v_ext[:, kt, HG * (gq // 2) + j, :],
                                           probs[:, (4 * gq + j) % RING, kt, :], start=(kt == 0), stop=(kt == TT - 1),
                                           skip_group_check=True)
                    mm.then_inc(s["probs_used"], 1)

                def to_tokens(b, gq, s=s):
                    after(pe, s["head_out_ready"], b, GQ, gq + 1 + 1)
                    after(pe, s["attn_ready"], b, GQ, gq + 2)
                    for i in range(2):
                        mm = pe.transpose(token_bank[:, P * i:P * i + P], head_out[:, gq % 2, P * i:P * i + P],
                                          ident[:, :])
                    mm.then_inc(s["token_ready"], 1)

                def turn(b, has_back, has_front, blk=blk):
                    for k in range(UNITS + 3):
                        if k < UNITS:
                            scores(b, k)
                        if k >= 10 and (k - 10) % 8 == 0:
                            release_group(b, (k - 10) // 8)
                        if 1 <= k <= UNITS:
                            turn_unit(b, k - 1)
                        if k >= 5 and (k - 5) % 4 == 0:
                            attend(b, (k - 5) // 4)
                        if k >= 6 and (k - 6) % 4 == 0:
                            to_tokens(b, (k - 6) // 4)
                        for piece, of in pieces(k, b, has_back, has_front):
                            dense(piece, of)

                def prologue():
                    for piece in ORDER:
                        if kind(piece) == 1:
                            dense(piece, 0)

                def epilogue():
                    for piece in ORDER:
                        if kind(piece) == -1:
                            dense(piece, B - 1)

                run(pe, prologue, turn, epilogue)

        @block.scalar
        def _(act):
            act.wait_ge(small_loaded, 16 * SMALL_LOADS)
            act.activation(cond_g[:, :, :], cond_t[:, :, :], ACT.Gelu_apprx_tanh).then_inc(cond_ready, 1)
            act.wait_ge(tp_ready, 2)
            for c in range(DC):
                act.activation(u_t[:, c, :], dense_bank[1][:, B * c:B * c + B], ACT.Silu,
                               bias=ada1_col[:, c:c + 1]).then_inc(silu_ready, 1)
            act.wait_ge(setup_done, 1)

            for blk, s in enumerate(S):
                act.wait_ge(w_loaded[blk], 16 * W_LOADS[blk])
                for wide, raw_w in ((w_qkv, raw_qkv), (w_out, raw_out), (w_up, raw_up)):
                    act.activation(wide[:, 0, :, :], raw_w, ACT.Copy).then_inc(w_high[blk], 1)

                def dense(piece, b, s=s, blk=blk):
                    name, i = piece
                    bank = dense_bank[bank_of(piece)]
                    if name in ("t1", "t2", "t3"):
                        piece_ready(act, s, piece, b)
                        high = (feat_a if name == "t1" else feat_m)[:, 0, i, :]
                        if blk == 0 and name != "t3":
                            factor, offset = ((ab[:, x, i, bass.ds(b, 1)] if name == "t1" else ln2_gb[:, x, i:i + 1])
                                              for x in range(2))
                            act.activation(feat_tmp[:, i, :], bank[:, :], ACT.Identity, scale=factor, bias=offset)\
                                .then_inc(used(s, piece), 1)
                            piece_read(act, s, piece, b)
                            act.activation(high, feat_tmp[:, i, :], ACT.Copy).then_inc(s[name + "_high"], 1)
                        else:
                            act.activation(high, bank[:, :], ACT.Copy).then_inc(s[name + "_high"], 1)
                    elif name == "qk":
                        piece_ready(act, s, piece, b)
                        if i == 0:
                            after(act, s["base_free"], b, 1, 1)
                        act.activation(qk_high[:, i, :], bank[:, :], ACT.Copy,
                                       scale=QUERY_SCALE if i % 2 == 0 else 1.0).then_inc(s["qk_high"], 1)
                    elif name == "v":
                        if i == 0:
                            if blk == 1:
                                after(act, s["col_ready"], b, 1, 1)
                            after(act, s["probs_used"], b, GQ, 1)
                        piece_ready(act, s, piece, b)
                        act.activation(v_ext[:, i, :, 0:HD], bank[:, 0:D].rearrange("p (h e) -> p h e", h=H),
                                       ACT.Copy, scale=1.0 if blk == 0 else mask_colf[:, i:i + 1])\
                            .then_inc(used(s, piece), 1)
                    elif name == "up":
                        piece_ready(act, s, piece, b)
                        act.activation(hidden[:, i, :], bank[:, :], ACT.Gelu_apprx_tanh if blk == 0 else ACT.Gelu,
                                       bias=up_bias[:, i:i + 1]).then_inc(used(s, piece), 1)

                def make_bias(b, u, s=s):
                    g, half, j = u // 8, u // 4 % 2, u % 4
                    h = HG * g + j
                    after(act, s["bias_used"], b, UNITS, u + 1)
                    act.activation(bias[:, u % 2, :, :], dist[:, 2 * half:2 * half + 2, :], ACT.Copy,
                                   scale=neg_scale[:, h:h + 1]).then_inc(s["bias_ready"], 1)

                def exps(b, u, s=s):
                    if u == 0:
                        after(act, s["probs_used"], b, GQ, 1)
                    elif u >= RING and (u - RING) % HG == 0:
                        after(act, s["probs_used"], b, GQ, 1 + (u - RING) // HG + 1)
                    for pair in range(2):
                        z = 2 * u + pair
                        after(act, s["turned_ready"], b, TILES, z + 1)
                        act.activation(probs[:, u % RING, 2 * pair:2 * pair + 2, :],
                                       turned_bank[z % 2][:, :].rearrange("p (a c) -> p a c", a=2), ACT.Exp)\
                            .then_inc(s["probs_ready"], 1)

                def take_out(b, gq, s=s):
                    after(act, s["probs_used"], b, GQ, gq + 1 + 1)
                    after(act, s["attn_ready"], b, GQ, gq + 1)
                    act.activation(head_out[:, gq % 2, :], pv_bank[:, 0:HALF], ACT.Copy)\
                        .then_inc(s["head_out_ready"], 1)

                def turn(b, has_back, has_front, blk=blk):
                    if blk == 0:
                        make_bias(b, 0)
                        make_bias(b, 1)
                    for k in range(UNITS + 3):
                        if blk == 0 and k + 2 < UNITS:
                            make_bias(b, k + 2)
                        if k < UNITS:
                            exps(b, k)
                        if k >= 5 and (k - 5) % 4 == 0:
                            take_out(b, (k - 5) // 4)
                        for piece, of in pieces(k, b, has_back, has_front):
                            dense(piece, of)

                def prologue():
                    for piece in ORDER:
                        if kind(piece) == 1:
                            dense(piece, 0)

                def epilogue():
                    for piece in ORDER:
                        if kind(piece) == -1:
                            dense(piece, B - 1)

                run(act, prologue, turn, epilogue)

        @block.vector
        def _(dve):
            steps = 0

            def step(ins):
                nonlocal steps
                steps += 1
                ins.then_inc(setup_step, 1)
                dve.wait_ge(setup_step, steps)

            dve.memset(no_bias[:, :], 0.0).then_inc(dve_consts, 1)
            step(dve.memset(v_ext[:, :, :, :], 0.0))
            dve.memset(v_ext[:, :, :, HD], 1.0).then_inc(dve_consts, 1)
            dve.memset(q_rows[KROWS:KROWS + 1, :, :, :].bitcast(F32), 1.0).then_inc(dve_consts, 1)
            for s in S:
                for name, n in (("base_free", 1), ("group_used", 2), ("scores_used", 2), ("bias_used", 2),
                                ("probs_ready", 2), ("probs_used", 1), ("head_out_ready", 1), ("attn_ready", 2),
                                ("dense_used0", 1), ("dense_used1", 1), ("y_ready", 1), ("y_stored", 16)):
                    dve.sem_inc(s[name], n)
            dve.wait_ge(small_loaded, 16 * SMALL_LOADS)
            step(dve.tensor_scalar_mul(neg_scale[:, :], neg_scale[:, :], -1.0))
            dve.wait_ge(tp_ready, 1)
            step(dve.tensor_tensor(tp[:, :, :], dense_bank[0][:, 0:4 * B].rearrange("p (c b) -> p c b", c=4),
                                   bt_col[:, :].unsqueeze(2).broadcast_to([P, 4, B]), ALU.add))
            step(dve.tensor_scalar_add(tp[:, 0:2, :], tp[:, 0:2, :], 1.0))
            step(dve.tensor_tensor(ab[:, 0, :, :], tp[:, 0:2, :],
                                   ln1_gb[:, 0, :].unsqueeze(2).broadcast_to([P, DC, B]), ALU.mult))
            step(dve.tensor_tensor(ab[:, 1, :, :], tp[:, 0:2, :],
                                   ln1_gb[:, 1, :].unsqueeze(2).broadcast_to([P, DC, B]), ALU.mult))
            step(dve.tensor_tensor(ab[:, 1, :, :], ab[:, 1, :, :], tp[:, 2:4, :], ALU.add))
            for c in range(3):
                dve.wait_ge(ada_ready, c + 1)
                bank = (score_bank[0], score_bank[1], turned_bank[0])[c]
                step(dve.tensor_tensor(ada[:, L * c:L * c + L], bank[0:B, :], ada2_bias[:, L * c:L * c + L], ALU.add))
            for n in range(2):
                shift, scale, gate = (ada[:, (3 * n + m) * D:(3 * n + m + 1) * D] for m in range(3))
                step(dve.scalar_tensor_tensor(out=mod_out[:, 2 * n * D:(2 * n + 1) * D], in0=scale, scalar=1.0,
                                              in1=gate, op0=ALU.add, op1=ALU.mult))
                step(dve.tensor_tensor(mod_out[:, (2 * n + 1) * D:(2 * n + 2) * D], shift, gate, ALU.mult))
            assert steps == SETUP_STEPS
            dve.wait_ge(setup_done, 1)

            for blk, s in enumerate(S):
                for n, (wide, raw_w) in enumerate(((w_qkv, raw_qkv), (w_out, raw_out), (w_up, raw_up))):
                    dve.wait_ge(w_high[blk], n + 1)
                    dve.tensor_tensor(wide[:, 1, :, :], raw_w, wide[:, 0, :, :].bitcast(F32), ALU.subtract)\
                        .then_inc(w_split[blk], 1)

                def norm_stats(b, n, src, s=s):
                    for t in range(TT):
                        ins = dve.bn_stats(stats[:, n, t, :], src[:, t, :])
                    ins.then_inc(s[f"stats_ready{n}"], 1)
                    after_alone(dve, s[f"stats_ready{n}"], b, 1, 1)
                    for t in range(TT):
                        ins = dve.bn_aggr(mean_var[:, n, t, :], stats[:, n, t, :])
                    ins.then_inc(s[f"mean_ready{n}"], 1)

                def norm_apply(b, n, src, s=s):
                    after(dve, s[f"rstd_ready{n}"], b, 1, 1)
                    for t in range(TT):
                        ins = dve.tensor_scalar(x_norm[:, t, :], src[:, t, :], mean_var[:, n, t, 0:1],
                                                rstd[:, n, t:t + 1], ALU.subtract, ALU.mult)
                    ins.then_inc(s[f"norm_ready{n}"], 1)

                def modulate(b, n, out_t, done, s=s):
                    after(dve, s[f"norm_ready{n}"], b, 1, 1)
                    dve.tensor_tensor(x_norm[:, :, :], x_norm[:, :, :],
                                      mod[:, 2 * n:2 * n + 1, :].broadcast_to([P, TT, D]), ALU.mult)\
                        .then_inc(s["scaled"], 1)
                    after(dve, s["scaled"], b, 2, n + 1)
                    after(dve, s[f"res_ready{n}"], b, 1, 1)
                    dve.tensor_tensor(out_t, x_norm[:, :, :], x_res[:, :, :], ALU.add).then_inc(s[done], 1)

                def norm(what, n, b, s=s, blk=blk):
                    if blk == 0 and n == 0:
                        if what == "stats":
                            after(dve, s["x_loaded"], b, 16, 16)
                            norm_stats(b, 0, x_in_t)
                        else:
                            if not isinstance(b, int) or b > 1:
                                after(dve, s["y_stored"], b, 16, -16)
                            norm_apply(b, 0, x_in_t)
                    elif blk == 0:
                        if what == "stats":
                            for t in range(2):
                                piece_read(dve, s, ("wout", 2 + t), b)
                            norm_stats(b, 1, x_res)
                        else:
                            if isinstance(b, int) and b + 2 >= B:
                                after(dve, s["y_stored"], b, 16, 16)
                            else:
                                piece_ready(dve, s, ("t1", DC - 1), b + 2)
                            norm_apply(b, 1, x_res)
                    elif n == 0:
                        if what == "stats":
                            for t in range(2):
                                piece_read(dve, s, ("wout", 2 + t), b)
                            norm_stats(b, 0, branch)
                        else:
                            after(dve, s["y_stored"], b, 16, 16)
                            norm_apply(b, 0, branch)
                            modulate(b, 0, x_res[:, :, :], "mid_ready")
                    else:
                        if what == "stats":
                            for t in range(2):
                                piece_read(dve, s, ("down", 2 + t), b)
                            norm_stats(b, 1, branch)
                        else:
                            norm_apply(b, 1, branch)
                            modulate(b, 1, x_norm[:, :, :], "y_ready")

                def dense(piece, b, s=s, blk=blk):
                    name, i = piece
                    bank = dense_bank[bank_of(piece)]
                    if name in ("t1", "t2", "t3"):
                        after(dve, s[name + "_high"], b, DC, i + 1)
                        feat = feat_a if name == "t1" else feat_m
                        if blk == 0 and name != "t3":
                            dve.tensor_tensor(feat[:, 1, i, :], feat_tmp[:, i, :], feat[:, 0, i, :].bitcast(F32),
                                              ALU.subtract).then_inc(s[name + "_low"], 1)
                        else:
                            dve.tensor_tensor(feat[:, 1, i, :], bank[:, :], feat[:, 0, i, :].bitcast(F32),
                                              ALU.subtract).then_inc(used(s, piece), 1)
                    elif name == "qk":
                        after(dve, s["qk_high"], b, 4, i + 1)
                        dve.scalar_tensor_tensor(out=qk_low[:, i, :], in0=bank[:, :],
                                                 scalar=QUERY_SCALE if i % 2 == 0 else 1.0,
                                                 in1=qk_high[:, i, :].bitcast(F32), op0=ALU.mult,
                                                 op1=ALU.subtract).then_inc(used(s, piece), 1)
                    elif name == "wout":
                        if i == 0 and blk == 0:
                            after(dve, s["res_loaded"], b, 16, 16)
                        piece_ready(dve, s, piece, b)
                        dst, other = (x_res[:, i, :], x_res[:, i, :]) if blk == 0 else (branch[:, i, :], out_bias[:, :])
                        dve.tensor_tensor(dst, other, bank[:, 0:D], ALU.add).then_inc(used(s, piece), 1)
                    elif name == "down":
                        if i == 0 and blk == 0:
                            after(dve, s["res_ready1"], b, 1, 1)
                        piece_ready(dve, s, piece, b)
                        dst, other = (x_norm[:, i, :], x_res[:, i, :]) if blk == 0 else (branch[:, i, :], down_bias[:, :])
                        dve.tensor_tensor(dst, other, bank[:, 0:D], ALU.add).then_inc(used(s, piece), 1)
                        if i == TT - 1 and blk == 0:
                            for t in range(2):
                                piece_read(dve, s, ("down", 2 + t), b)
                            dve.sem_inc(s["y_ready"], 1)

                def shift_scores(b, u, s=s, blk=blk):
                    if blk == 0:
                        after(dve, s["bias_ready"], b, UNITS, u + 1)
                    for i in range(2):
                        t = 2 * u + i
                        after_alone(dve, s["scores_ready"], b, TILES, t + 1)
                        dve.tensor_tensor_reduce(shifted[:, u % 2, i, :], score_bank[t % 2][:, :],
                                                 bias[:, u % 2, i, :] if blk == 0 else no_bias[:, :],
                                                 1.0, -3.0e38, ALU.add, ALU.max, row_max[:, t % 4:t % 4 + 1])\
                            .then_inc(s["scores_used"], 1)
                    for i in range(2):
                        t = 2 * u + i
                        after(dve, s["scores_used"], b, TILES, t + 1 + 2)
                        ins = dve.tensor_scalar(shifted[:, u % 2, i, :], shifted[:, u % 2, i, :],
                                                row_max[:, t % 4:t % 4 + 1], None, ALU.subtract)
                        ins.then_inc(s["bias_used"] if i == 0 else s["shifted_ready"], 1)

                def divide(b, gq, s=s):
                    after(dve, s["token_ready"], b, GQ, gq + 1)
                    heads = token_bank[:, 0:2 * P].rearrange("p (i j e) -> p i j e", i=2, e=SLOT)
                    dve.reciprocal(inv_sum[:, :, :], heads[:, :, :, HD]).then_inc(s["inv_ready"], 1)
                    after(dve, s["inv_ready"], b, GQ, gq + 1)
                    g, t0 = gq // 2, 2 * (gq % 2)
                    for i in range(2):
                        ins = dve.tensor_tensor(attn[:, t0 + i, HG * HD * g:HG * HD * (g + 1)]
                                                .rearrange("p (j e) -> p j e", j=HG), heads[:, i, :, 0:HD],
                                                inv_sum[:, i, :].unsqueeze(2).broadcast_to([P, HG, HD]), ALU.mult)
                    ins.then_inc(s["attn_ready"], 1)

                def turn(b, has_back, has_front, blk=blk, s=s):
                    for k in range(UNITS + 3):
                        if k < UNITS:
                            shift_scores(b, k)
                        if k >= 7 and (k - 7) % 4 == 0:
                            if k == 7 and has_back:
                                piece_ready(dve, s, ("t3", DC - 1), b - 1)
                            divide(b, (k - 7) // 4)
                        for piece, of in pieces(k - 1, b, has_back, has_front):
                            dense(piece, of)
                        if k in NORM_STEP[blk]:
                            what, n = NORM_STEP[blk][k]
                            ahead = blk == 0 and n == 0
                            if has_front if ahead else has_back:
                                norm(what, n, b + 1 if ahead else b - 1)
                    divide(b, GQ - 1)

                def prologue(blk=blk):
                    if blk == 0:
                        norm("stats", 0, 0)
                        norm("norm", 0, 0)
                    for piece in ORDER:
                        if kind(piece) == 1:
                            dense(piece, 0)

                def epilogue(blk=blk):
                    for piece in ORDER:
                        if kind(piece) == -1:
                            dense(piece, B - 1)
                            if piece == ("wout", TT - 1):
                                n = 1 if blk == 0 else 0
                                norm("stats", n, B - 1)
                                norm("norm", n, B - 1)
                    if blk == 1:
                        norm("stats", 1, B - 1)
                        norm("norm", 1, B - 1)

                run(dve, prologue, turn, epilogue)


SMALL_LOADS = 14
POOL_CONSTS = 3
DVE_CONSTS = 3
SETUP_STEPS = 2 + 5 + 3 + 4

_INS = ['x', 'cond_1024', 'mask_BxS_bf1', 'mask_BxS_bk0', 'L0_cond_torus_dist', 'L0_cond_ln1_g', 'L0_cond_ln1_b',
        'L0_cond_Wqkv', 'L0_cond_Wout', 'L0_cond_torus_scale', 'L0_cond_ln2_g', 'L0_cond_ln2_b', 'L0_cond_W1',
        'L0_cond_b1', 'L0_cond_W2', 'L0_cond_b2', 'L0_cond_Wt', 'L0_cond_bt', 'L1_cond_qkv_w', 'L1_cond_proj_w',
        'L1_cond_proj_b', 'L1_cond_fc1_w', 'L1_cond_fc1_b', 'L1_cond_fc2_w', 'L1_cond_fc2_b', 'L1_cond_ada1_w',
        'L1_cond_ada1_b', 'L1_cond_ada2_w', 'L1_cond_ada2_b']


def kernel(**inputs):
    import numpy as np
    import concourse.bacc as bacc
    from concourse.bass_utils import run_bass_kernel_spmd

    nc = bacc.Bacc("TRN2", target_bir_lowering=False, num_devices=1)
    arrays, d = {}, {}
    for name in _INS:
        a = np.ascontiguousarray(inputs[name])
        arrays[f"in_{name}"] = a
        d[name] = nc.dram_tensor(f"in_{name}", a.shape, mybir.dt.from_np(a.dtype), kind="ExternalInput").ap()
    out = nc.dram_tensor("out", inputs["x"].shape, F32, kind="ExternalOutput").ap()
    build(nc, d, out)
    r = run_bass_kernel_spmd(nc, [arrays], core_ids=[0])
    return r.results[0]["out"]
```

```python
from contextlib import ExitStack

import concourse.bass as bass
from concourse import mybir

ALU = mybir.AluOpType
ACT = mybir.ActivationFunctionType
F32 = mybir.dt.float32
F32R = mybir.dt.float32r
U8 = mybir.dt.uint8
I32 = mybir.dt.int32

P = 128
EPS = 1e-5
PAD = 1e30
QUERY_SCALE = 0.25


def build(nc, d, out):
    B, L, D = d["x"].shape
    H = d["L0_cond_torus_scale"].shape[0]
    F = d["L0_cond_W1"].shape[1]
    HD = D // H
    TT = L // P
    DC = D // P
    FCH = F // P
    HG = 4
    G = H // HG
    SLOT = P // HG
    KROWS = 4 * HD
    UNITS = 2 * H
    HALF = L // 2
    GQ = 2 * G
    TILES = 2 * UNITS
    RING = 6
    EARLY = L - P
    assert HD == 16 and TT == 4 and DC == 2 and G == 4 and FCH == 8

    AT_STEP = [
        {0: [("v", 0)], 1: [("v", 1)], 2: [("t3", 0), ("t3", 1)], 4: [("v", 2)], 5: [("v", 3), ("t1", 0)],
         6: [("t1", 1)], 7: [("wout", 0)], 8: [("wout", 1)], 9: [("wout", 2)], 10: [("wout", 3)],
         11: [("qk", 0)], 12: [("qk", 1)], 13: [("qk", 2)], 14: [("qk", 3)], 15: [("t2", 0), ("t2", 1)],
         17: [("up", 0), ("up", 1)], 19: [("up", 2), ("up", 3)], 21: [("up", 4), ("up", 5)],
         23: [("up", 6), ("up", 7)], 27: [("down", 0)], 30: [("down", 1)], 32: [("down", 2)], 35: [("down", 3)]},
        {0: [("v", 0), ("v", 1)], 1: [("t3", 0), ("t3", 1)], 3: [("wout", 0)], 4: [("wout", 1)], 5: [("wout", 2)],
         6: [("wout", 3), ("v", 2)], 7: [("v", 3)], 8: [("t1", 0), ("t1", 1)], 10: [("qk", 0)],
         11: [("qk", 1)], 13: [("t2", 0), ("t2", 1)], 15: [("up", 0), ("up", 1)], 17: [("up", 2), ("up", 3)],
         19: [("qk", 2)], 20: [("qk", 3)], 21: [("up", 4), ("up", 5)], 23: [("up", 6), ("up", 7)],
         26: [("down", 0)], 28: [("down", 1)], 30: [("down", 2)], 32: [("down", 3)]}]
    STEPS = UNITS + 5
    DOWN_STEP = [{25: (0, 2), 26: (2, 5), 27: (5, 8), 28: (8, 12), 29: (12, 14), 30: (14, 17), 31: (17, 20),
                  32: (20, 24), 33: (24, 26), 34: (26, 29), 35: (29, 32)},
                 {25 + n: (4 * n, 4 * n + 4) for n in range(FCH)}]
    TURN = 2
    ATTEND = [(0, 1, 6), (1, 3, 7), (3, 4, 8)]
    OUT = 8
    NORM_STEP = [{2: [("stats", 0)], 4: [("norm", 0)], 11: [("stats", 1)], 13: [("norm", 1)]},
                 {7: [("stats", 0)], 9: [("norm", 0)], 33: [("stats", 1)], 35: [("norm", 1)]}]
    FRONT = ("t1", "qk")
    BACK = ("t3", "wout", "t2", "up", "down")
    ORDER = [[p for k in range(STEPS) for p in AT_STEP[blk].get(k, [])] for blk in range(2)]
    ND = len(ORDER[0])
    assert ND % 2 == 0 and set(ORDER[0]) == set(ORDER[1])

    def kind(piece):
        return -1 if piece[0] in BACK else 1 if piece[0] in FRONT else 0

    PLACE = []
    for order in ORDER:
        passed = [(p, 0) for p in order if kind(p) == 1]
        for turn in range(B):
            passed += [(p, turn + kind(p)) for p in order if 0 <= turn + kind(p) < B]
        passed += [(p, B - 1) for p in order if kind(p) == -1]
        PLACE.append({x: n for n, x in enumerate(passed)})

    def place(blk, piece, b):
        if isinstance(b, int):
            return PLACE[blk][piece, b]
        return PLACE[blk][piece, 2] - 2 * ND + b * ND

    for blk in range(2):
        for p in ORDER[blk]:
            for turn in range(1, B - 1):
                b = turn + kind(p)
                assert PLACE[blk][p, b] == PLACE[blk][p, 2] + (b - 2) * ND, p
            assert len({PLACE[blk][p, b] % 2 for b in range(B)}) == 1

    def bank_of(blk, piece):
        return PLACE[blk][piece, 2] % 2

    with ExitStack() as ctx:
        def sb(name, shape, dt=F32):
            return ctx.enter_context(nc.sbuf_tensor(name, shape, dt))

        def sem(name):
            return ctx.enter_context(nc.semaphore(name))

        def dram(name, shape):
            return nc.dram_tensor(name, shape, F32, kind="Internal").ap()

        x_mid = dram("x_mid", (B, L, D))
        qk_halves = dram("qk_halves", (2, B, 2, 2, D, L))
        mod_rows = dram("mod_rows", (B, 4 * D))

        flags = nc.dram_tensor("flags", (1, B), I32, kind="Internal").ap()

        score_bank = [ctx.enter_context(nc.psum_tensor(f"score{i}", [P, L], F32)) for i in range(2)]
        turned_bank = [ctx.enter_context(nc.psum_tensor(f"turned{i}", [P, L], F32)) for i in range(2)]
        pv_bank = ctx.enter_context(nc.psum_tensor("pv", [P, L], F32))
        token_bank = ctx.enter_context(nc.psum_tensor("token", [P, L], F32))
        dense_bank = [ctx.enter_context(nc.psum_tensor(f"dense{i}", [P, L], F32)) for i in range(2)]

        w_qkv = sb("w_qkv", [P, 2, DC, 3 * D], F32R)
        w_out = sb("w_out", [P, 2, DC, D], F32R)
        w_up = sb("w_up", [P, 2, DC, F], F32R)
        w_down = sb("w_down", [P, FCH, D])
        up_bias = sb("up_bias", [P, FCH])
        down_bias = sb("down_bias", [P, D])
        out_bias = sb("out_bias", [P, D])
        ident = sb("ident", [P, P])
        minus_half = sb("minus_half", [P, TT])
        neg_scale = sb("neg_scale", [P, H])
        dist = sb("dist", [P, TT, L])
        no_bias = sb("no_bias", [P, L])
        ln2_gb = sb("ln2_gb", [P, 2, DC])
        ab = sb("ab", [P, 2, DC, B])
        x_in_t = sb("x_in_t", [P, TT, D])
        x_res = sb("x_res", [P, TT, D])
        x_norm = sb("x_norm", [P, TT, D])
        branch = dist[:, 0:2, :].rearrange("p a (c n) -> p (a c) n", n=D)
        mod = dist[:, 2:4, :].rearrange("p a (c n) -> p (a c) n", n=D)
        feat_a = sb("feat_a", [P, 2, DC, L], F32R)
        feat_m = sb("feat_m", [P, 2, DC, L], F32R)
        qk_high = sb("qk_high", [P, 4, L], F32R)
        qk_low = sb("qk_low", [P, 4, L], F32R)
        q_rows = sb("q_rows", [KROWS + 1, 2, HG, L], F32R)
        k_rows = sb("k_rows", [KROWS + 1, 2, HG, L], F32R)
        v_ext = sb("v_ext", [P, TT, H, SLOT])
        bias = sb("bias", [P, 2, 2, L])
        shifted = sb("shifted", [P, 3, 2, L])
        probs = sb("probs", [P, RING, TT, HALF])
        head_out = sb("head_out", [P, 2, HALF])
        inv_sum = sb("inv_sum", [P, 2, HG])
        attn = sb("attn", [P, TT, D])
        hidden = sb("hidden", [P, FCH, L])
        feat_tmp = hidden[:, FCH - DC:FCH, :]
        row_max = sb("row_max", [P, 4])
        stats = sb("stats", [P, 2, TT, 6])
        mean_var = sb("mean_var", [P, 2, TT, 2])
        var_eps = sb("var_eps", [P, 2, TT])
        rstd = sb("rstd", [P, 2, TT])
        mask_row = sb("mask_row", [KROWS + 1, L], U8)
        mask_neg = sb("mask_neg", [KROWS + 1, L], F32R)
        mask_col = sb("mask_col", [P, TT], U8)
        mask_colf = sb("mask_colf", [P, TT])
        early_max = sb("early_max", [1, B])
        early_flag = sb("early_flag", [1, B], I32)
        cond_t = sb("cond_t", [P, DC, B])
        cond_g = sb("cond_g", [P, DC, B])
        u_t = sb("u_t", [P, DC, B])
        tp = sb("tp", [P, 4, B])
        bt_col = sb("bt_col", [P, 4])
        ada1_col = sb("ada1_col", [P, DC])
        ln1_gb = sb("ln1_gb", [P, 2, DC])
        raw = hidden[:, :, :].rearrange("p a b -> p (a b)")
        ada2 = raw[:, 0:3072].rearrange("p (c n) -> p c n", c=DC)
        w_t = raw[:, 3072:4096].rearrange("p (c n) -> p c n", c=DC)
        ada1 = x_in_t[:, 0:2, :]
        early = shifted[0:B, 0:2, :, :].rearrange("p a b c -> p (a b c)")
        ada2_bias = early[:, 0:1536]
        ada = bias[0:B, :, :, :].rearrange("p a b c -> p (a b c)")[:, 0:1536]
        all_masks = probs[0:1, RING - 1, :, :].rearrange("p a b -> p (a b)").bitcast(U8)[:, 0:B * L]\
            .rearrange("p (b l) -> p b l", b=B)
        mod_out = x_res[0:B, :, :].rearrange("p a b -> p (a b)")
        staged = probs[:, :, :, :].rearrange("p a b c -> p (a b c)")
        raw_qkv = staged[:, 0:1536].rearrange("p (c n) -> p c n", c=DC)
        raw_out = staged[:, 1536:2048].rearrange("p (c n) -> p c n", c=DC)
        raw_up = staged[:, 2048:4096].rearrange("p (c n) -> p c n", c=DC)

        small_loaded = sem("small_loaded")
        raw_loaded = [sem("raw_loaded0"), sem("raw_loaded1")]
        w_loaded = [sem("w_loaded0"), sem("w_loaded1")]
        w_high = [sem("w_high0"), sem("w_high1")]
        w_split = [sem("w_split0"), sem("w_split1")]
        pool_consts = sem("pool_consts")
        dve_consts = sem("dve_consts")
        cond_ready = sem("cond_ready")
        tp_ready = sem("tp_ready")
        silu_ready = sem("silu_ready")
        ada_ready = sem("ada_ready")
        setup_step = sem("setup_step")
        mod_stored = sem("mod_stored")
        setup_done = sem("setup_done")
        carried = sem("carried")
        S = []
        for blk in range(2):
            n = {"blk": blk}
            for name in ("x_loaded", "res_loaded", "mask_loaded", "mask_ready", "col_loaded", "col_ready",
                         "vmask_ready", "mod_loaded", "halves_stored0", "halves_stored1", "base_free",
                         "group0_loaded", "group1_loaded", "group_used", "scores_ready", "scores_used",
                         "bias_ready", "bias_used", "shifted_ready", "turned_ready", "probs_ready", "probs_used",
                         "head_out_ready", "token_ready", "inv_ready", "attn_ready", "dense_ready",
                         "dense_used0", "dense_used1", "t1_high", "t2_high", "t3_high", "qk_high", "t1_low", "t2_low",
                         "stats_ready0", "stats_ready1",
                         "mean_ready0", "mean_ready1", "var_ready0", "var_ready1", "rstd_ready0", "rstd_ready1",
                         "norm_ready0", "norm_ready1", "mid_ready", "res_ready0", "res_ready1", "scaled",
                         "y_ready", "y_stored"):
                n[name] = sem(f"b{blk}_{name}")
            S.append(n)

        def after(eng, s, b, per_batch, n):
            eng.wait_ge(s, b * per_batch + n)

        def after_alone(eng, s, b, per_batch, n):
            eng.wait_ge(s, b * per_batch + n)
            eng.sem_inc(carried, 1)

        def used(s, piece):
            return (s["dense_used0"], s["dense_used1"])[bank_of(s["blk"], piece)]

        def count_in_bank(s, piece, b):
            n = PLACE[s["blk"]]
            if isinstance(b, int):
                return n[piece, b] // 2
            return n[piece, 2] // 2 - ND + b * (ND // 2)

        def bank_free(eng, s, piece, b):
            eng.wait_ge(used(s, piece), count_in_bank(s, piece, b) + 1)

        def piece_read(eng, s, piece, b):
            eng.wait_ge(used(s, piece), count_in_bank(s, piece, b) + 2)

        def halves_ready(eng, s, blk, name, b):
            if blk == 0 and name != "t3":
                after(eng, s[name + "_low"], b, DC, DC)
            else:
                for c in range(DC):
                    piece_read(eng, s, (name, c), b)

        def piece_ready(eng, s, piece, b):
            eng.wait_ge(s["dense_ready"], place(s["blk"], piece, b) + 1)

        def run(eng, blk, prologue, turn, epilogue):
            prologue()
            by_mask(eng, blk, 0, turn, False, True)
            with eng.Fori(1, B - 1) as b:
                by_mask(eng, blk, b, turn, True, True)
            by_mask(eng, blk, B - 1, turn, True, False)
            epilogue()

        def by_mask(eng, blk, b, turn, *has):
            if blk == 0:
                turn(b, *has, False)
                return
            flag = eng.value_load(flags[0:1, bass.ds(b, 1)], min_val=0, max_val=1)
            with eng.If(flag > 0):
                turn(b, *has, False)
            with eng.Else():
                turn(b, *has, True)

        def pieces(blk, k, b, has_back, has_front):
            for p in AT_STEP[blk].get(k, []):
                if {-1: has_back, 0: True, 1: has_front}[kind(p)]:
                    yield p, b + kind(p)

        block = ctx.enter_context(nc.Block())
        RAW_LOADS, W_LOADS = 3, 4

        @block.sync
        def _(sp):
            def load_small(dst, src):
                sp.dma_start(dst, src).then_inc(small_loaded, 16)

            def load_raw_weights(blk, pre, qkv, wout, up):
                for dst, name in ((raw_qkv, qkv), (raw_out, wout), (raw_up, up)):
                    sp.dma_start(dst, d[pre + name].rearrange("(c p) n -> p c n", p=P)).then_inc(raw_loaded[blk], 16)

            def load_weights(blk, pre, up_b, down, down_b):
                for dst, src in ((w_down[:, :, :], d[pre + down].rearrange("(c p) n -> p c n", p=P)),
                                 (up_bias[:, :], d[pre + up_b].rearrange("(c p) -> p c", p=P)),
                                 (down_bias[:, :], d[pre + down_b].unsqueeze(0).broadcast_to([P, D])),
                                 (out_bias[:, :], d["L1_cond_proj_b"].unsqueeze(0).broadcast_to([P, D]))):
                    sp.dma_start(dst, src).then_inc(w_loaded[blk], 16)

            with nc.allow_non_contiguous_dma(reason="small vectors laid on partitions"):
                load_small(cond_t[:, 0, :], d["cond_1024"][:, 0:P].rearrange("b p -> p b"))
                load_small(cond_t[:, 1, :], d["cond_1024"][:, P:D].rearrange("b p -> p b"))
                load_small(w_t, d["L0_cond_Wt"].rearrange("(c p) n -> p c n", p=P))
                load_small(bt_col[:, :], d["L0_cond_bt"].rearrange("(c p) -> p c", p=P))
                load_small(ln1_gb[:, 0, :], d["L0_cond_ln1_g"].rearrange("(c p) -> p c", p=P))
                load_small(ln1_gb[:, 1, :], d["L0_cond_ln1_b"].rearrange("(c p) -> p c", p=P))
                load_small(ln2_gb[:, 0, :], d["L0_cond_ln2_g"].rearrange("(c p) -> p c", p=P))
                load_small(ln2_gb[:, 1, :], d["L0_cond_ln2_b"].rearrange("(c p) -> p c", p=P))
                load_small(ada1, d["L1_cond_ada1_w"].rearrange("(c p) n -> p c n", p=P))
                load_small(ada1_col[:, :], d["L1_cond_ada1_b"].rearrange("(c p) -> p c", p=P))
                load_small(ada2, d["L1_cond_ada2_w"].rearrange("(c p) n -> p c n", p=P))
                load_small(ada2_bias, d["L1_cond_ada2_b"].unsqueeze(0).broadcast_to([B, 6 * D]))
                load_small(all_masks, d["mask_BxS_bk0"].unsqueeze(0))
                load_small(neg_scale[:, :], d["L0_cond_torus_scale"].unsqueeze(0).broadcast_to([P, H]))
                load_small(dist[:, :, :], d["L0_cond_torus_dist"][0].rearrange("(t p) k -> p t k", p=P))
                load_raw_weights(0, "L0_cond_", "Wqkv", "Wout", "W1")
                load_weights(0, "L0_cond_", "b1", "W2", "b2")
                sp.wait_ge(dve_consts, DVE_CONSTS)
                sp.wait_ge(pool_consts, POOL_CONSTS)
                sp.wait_ge(setup_step, SETUP_STEPS)
                sp.dma_start(mod_rows, mod_out).then_inc(mod_stored, 16)
                sp.dma_start(flags, early_flag[:, :]).then_inc(mod_stored, 16)
                sp.wait_ge(mod_stored, 32)
                sp.sem_inc(setup_done, 1)

                for blk, s in enumerate(S):
                    x_src = (d["x"], x_mid)[blk]
                    y_dst = (x_mid, out)[blk]
                    mask = (d["mask_BxS_bf1"], d["mask_BxS_bk0"])[blk]

                    def load_x(b, s=s, x_src=x_src):
                        sp.dma_start(x_in_t[:, :, :], x_src[b].rearrange("(t p) n -> p t n", p=P))\
                            .then_inc(s["x_loaded"], 16)

                    def load_res(b, s=s, x_src=x_src):
                        sp.dma_start(x_res[:, :, :], x_src[b].rearrange("(t p) n -> p t n", p=P))\
                            .then_inc(s["res_loaded"], 16)

                    def load_mod(b, s=s):
                        sp.dma_start(mod.rearrange("p a n -> p (a n)"),
                                     mod_rows[b].unsqueeze(0).broadcast_to([P, 4 * D])).then_inc(s["mod_loaded"], 16)

                    def load_mask(b, s=s, mask=mask, blk=blk):
                        sp.dma_start(mask_row[KROWS:KROWS + 1, :], mask[bass.ds(b, 1), :])\
                            .then_inc(s["mask_loaded"], 16)
                        if blk == 1:
                            sp.dma_start(mask_col[:, :], mask[b].rearrange("(t p) -> p t", p=P))\
                                .then_inc(s["col_loaded"], 16)

                    def store_halves(b, s=s, blk=blk):
                        for c in range(4):
                            piece_read(sp, s, ("qk", c), b)
                            sp.sem_inc(carried, 1)
                            rows = slice(P * (c // 2), P * (c // 2) + P)
                            stored = (s["halves_stored0"], s["halves_stored1"])[c // 2]
                            sp.dma_start(qk_halves[blk, b, 0, c % 2, rows, :], qk_high[:, c, :].bitcast(F32))\
                                .then_inc(stored, 16)
                            sp.dma_start(qk_halves[blk, b, 1, c % 2, rows, :], qk_low[:, c, :].bitcast(F32))\
                                .then_inc(stored, 16)

                    def load_group(b, g, s=s, blk=blk):
                        after_alone(sp, (s["halves_stored0"], s["halves_stored1"])[g // 2], b, 64, 64)
                        if g == 2:
                            sp.sem_inc(s["base_free"], 1)
                        after_alone(sp, s["mask_ready"], b, 1, 1)
                        after_alone(sp, s["group_used"], b, G, g + 1)
                        loaded = (s["group0_loaded"], s["group1_loaded"])[g % 2]
                        rows = slice(HG * HD * g, HG * HD * (g + 1))
                        for r in range(4):
                            sp.dma_start(q_rows[HD * r:HD * r + HD, g % 2, :, :].bitcast(F32),
                                         qk_halves[blk, b, r // 2, 0, rows, :]
                                         .rearrange("(h e) n -> e h n", e=HD)).then_inc(loaded, 16)
                            sp.dma_start(k_rows[HD * r:HD * r + HD, g % 2, :, :].bitcast(F32),
                                         qk_halves[blk, b, r % 2, 1, rows, :]
                                         .rearrange("(h e) n -> e h n", e=HD)).then_inc(loaded, 16)
                        sp.dma_start(k_rows[KROWS:KROWS + 1, g % 2, :, :].bitcast(F32),
                                     mask_neg[KROWS:KROWS + 1, :].bitcast(F32).unsqueeze(1)
                                     .broadcast_to([1, HG, L])).then_inc(loaded, 16)

                    def store_y(b, s=s, y_dst=y_dst):
                        after_alone(sp, s["y_ready"], b, 1, 2)
                        sp.dma_start(y_dst[b].rearrange("(t p) n -> p t n", p=P), x_norm[:, :, :])\
                            .then_inc(s["y_stored"], 16)

                    def prologue(s=s, blk=blk):
                        load_x(0)
                        load_mask(0)
                        store_halves(0)
                        load_group(0, 0)
                        load_group(0, 1)

                    def turn(b, has_back, has_front, short, s=s, blk=blk):
                        if has_back:
                            after_alone(sp, s["y_ready"], b, 1, 0)
                            load_res(b - 1)
                            if blk == 1:
                                load_mod(b - 1)
                        if has_front:
                            if blk == 0:
                                after_alone(sp, s["norm_ready0"], b, 1, 1)
                            load_x(b + 1)
                        load_group(b, 2)
                        load_group(b, 3)
                        if has_front:
                            after_alone(sp, s["group1_loaded"], b, 2 * 9 * 16, 2 * 9 * 16)
                            after_alone(sp, s["group0_loaded"], b, 2 * 9 * 16, 2 * 9 * 16)
                            if blk == 1:
                                after_alone(sp, s["vmask_ready"], b, 1, 1)
                            load_mask(b + 1)
                            store_halves(b + 1)
                            load_group(b + 1, 0)
                        if has_back:
                            store_y(b - 1)
                        if has_front:
                            load_group(b + 1, 1)

                    def epilogue(s=s, blk=blk):
                        sp.wait_ge(s["y_ready"], B)
                        load_res(B - 1)
                        if blk == 1:
                            load_mod(B - 1)
                        if blk == 0:
                            sp.wait_ge(s["probs_used"], GQ * B + 1)
                            load_raw_weights(1, "L1_cond_", "qkv_w", "proj_w", "fc1_w")
                        store_y(B - 1)
                        sp.wait_ge(s["y_stored"], 16 * (B + 1))
                        if blk == 0:
                            load_weights(1, "L1_cond_", "fc1_b", "fc2_w", "fc2_b")

                    run(sp, 0, prologue, turn, epilogue)

        @block.gpsimd
        def _(pool):
            pool.memset(ident[:, :], 0.0).then_inc(pool_consts, 1)
            pool.memset(minus_half[:, :], -0.5).then_inc(pool_consts, 1)
            pool.wait_ge(pool_consts, 1)
            pool.affine_select(out=ident[:, :], in_=ident[:, :], compare_op=ALU.not_equal, fill=1.0, base=0,
                               pattern=[[-1, P]], channel_multiplier=1).then_inc(pool_consts, 1)
            pool.wait_ge(setup_done, 1)

            for blk, s in enumerate(S):
                def inverse_std(b, n, s=s):
                    after_alone(pool, s[f"mean_ready{n}"], b, 1, 1)
                    pool.tensor_scalar_add(var_eps[:, n, :], mean_var[:, n, :, 1], EPS).then_inc(s[f"var_ready{n}"], 1)
                    after(pool, s[f"var_ready{n}"], b, 1, 1)
                    pool.tensor_tensor(rstd[:, n, :], var_eps[:, n, :], minus_half[:, :], ALU.pow)\
                        .then_inc(s[f"rstd_ready{n}"], 1)
                    after_alone(pool, s[f"rstd_ready{n}"], b, 1, 1)

                def mask(b, s=s, blk=blk):
                    after_alone(pool, s["mask_loaded"], b, 16, 16)
                    pool.tensor_scalar(mask_neg[KROWS:KROWS + 1, :], mask_row[KROWS:KROWS + 1, :], PAD, -PAD,
                                       ALU.mult, ALU.add).then_inc(s["mask_ready"], 1)
                    after_alone(pool, s["mask_ready"], b, 1, 1)

                def value_mask(b, s=s):
                    after_alone(pool, s["probs_used"], b, GQ, 1)
                    after_alone(pool, s["col_loaded"], b, 16, 16)
                    pool.tensor_copy(mask_colf[:, :], mask_col[:, :]).then_inc(s["col_ready"], 1)
                    after_alone(pool, s["col_ready"], b, 1, 1)
                    pool.tensor_copy(v_ext[:, :, :, HD], mask_colf[:, :].unsqueeze(2).broadcast_to([P, TT, H]))\
                        .then_inc(s["vmask_ready"], 1)

                def add_bias(b, s=s):
                    after(pool, s["norm_ready1"], b, 1, 1)
                    pool.tensor_tensor(x_res[:, :, :], x_res[:, :, :],
                                       down_bias[:, :].unsqueeze(1).broadcast_to([P, TT, D]), ALU.add)\
                        .then_inc(s["res_ready1"], 1)
                    after_alone(pool, s["res_ready1"], b, 1, 1)

                def add_shift(b, n, s=s):
                    if n == 0:
                        after(pool, s["res_loaded"], b, 16, 16)
                        after(pool, s["mod_loaded"], b, 16, 16)
                    else:
                        piece_ready(pool, s, ("t2", DC - 1), b)
                    pool.tensor_tensor(x_res[:, :, :], x_res[:, :, :],
                                       mod[:, 2 * n + 1:2 * n + 2, :].broadcast_to([P, TT, D]), ALU.add)\
                        .then_inc(s[f"res_ready{n}"], 1)
                    after_alone(pool, s[f"res_ready{n}"], b, 1, 1)

                def back(b, has_front, blk=blk):
                    if blk == 0:
                        inverse_std(b, 1)
                        add_bias(b)
                    else:
                        add_shift(b, 0)
                        inverse_std(b, 0)
                        add_shift(b, 1)
                    if has_front:
                        mask(b + 2)
                    if blk == 1:
                        inverse_std(b, 1)

                def prologue(blk=blk):
                    mask(0)
                    if blk == 0:
                        inverse_std(0, 0)

                def turn(b, has_back, has_front, short, blk=blk):
                    if blk == 1:
                        value_mask(b)
                    if has_front and blk == 0:
                        inverse_std(b + 1, 0)
                    if has_back:
                        back(b - 1, has_front)
                    else:
                        mask(b + 1)

                run(pool, 0, prologue, turn, lambda: back(B - 1, False))

        @block.tensor
        def _(pe):
            pe.wait_ge(small_loaded, 16 * SMALL_LOADS)
            pe.wait_ge(cond_ready, 1)
            for c in range(4):
                for k in range(DC):
                    mm = pe.matmul(dense_bank[0][:, B * c:B * c + B], w_t[:, k, P * c:P * c + P], cond_g[:, k, :],
                                   start=(k == 0), stop=(k == DC - 1))
            mm.then_inc(tp_ready, 1)
            for c in range(DC):
                for k in range(DC):
                    mm = pe.matmul(dense_bank[1][:, B * c:B * c + B], ada1[:, k, P * c:P * c + P], cond_t[:, k, :],
                                   start=(k == 0), stop=(k == DC - 1))
            mm.then_inc(tp_ready, 1)
            pe.wait_ge(silu_ready, DC)
            for c in range(3):
                bank = (score_bank[0], score_bank[1], turned_bank[0])[c]
                for k in range(DC):
                    mm = pe.matmul(bank[0:B, :], u_t[:, k, :], ada2[:, k, L * c:L * c + L],
                                   start=(k == 0), stop=(k == DC - 1))
                mm.then_inc(ada_ready, 1)
            pe.wait_ge(setup_done, 1)

            def products(out_ap, pairs):
                terms = [(left[x], right[y]) for left, right in pairs for x, y in ((0, 0), (0, 1), (1, 0))]
                for n, (left, right) in enumerate(terms):
                    mm = pe.matmul(out_ap, left, right, start=(n == 0), stop=(n == len(terms) - 1))
                return mm

            for blk, s in enumerate(S):
                pe.wait_ge(w_split[blk], 3)

                def halves(t, c, cols):
                    return [t[:, x, c, cols] for x in range(2)]

                def transposes(bank, src, c):
                    for t in range(TT):
                        mm = pe.transpose(bank[:, P * t:P * t + P], src[:, t, P * c:P * c + P], ident[:, :])
                    return mm

                def down_chunks(b, first, last, s=s, blk=blk):
                    for n in range(first, last):
                        i, c = n // FCH, n % FCH
                        piece = ("down", i)
                        if n == 0:
                            for m in range(2):
                                piece_read(pe, s, ("up", FCH - 2 + m), b)
                        if c == 0:
                            bank_free(pe, s, piece, b)
                        mm = pe.matmul(dense_bank[bank_of(blk, piece)][:, 0:D], hidden[:, c, P * i:P * i + P],
                                       w_down[:, c, :], start=(c == 0), stop=(c == FCH - 1))
                        if c == FCH - 1:
                            mm.then_inc(s["dense_ready"], 1)

                def dense(piece, b, s=s, blk=blk):
                    name, i = piece
                    bank = dense_bank[bank_of(blk, piece)]
                    if name == "down":
                        return
                    tokens = slice(P * i, P * i + P)
                    every = slice(0, L)
                    if name == "t1":
                        if blk == 0:
                            after(pe, s["norm_ready0"], b, 1, 1)
                        else:
                            after(pe, s["x_loaded"], b, 16, 16)
                    elif name == "qk" and i == 0:
                        halves_ready(pe, s, blk, "t1", b)
                    elif name == "t3":
                        after(pe, s["attn_ready"], b, GQ, GQ + 2)
                    elif name == "wout" and i == 0:
                        halves_ready(pe, s, blk, "t3", b)
                    elif name == "t2":
                        after(pe, s["norm_ready1" if blk == 0 else "mid_ready"], b, 1, 1)
                    elif name == "up" and i == 0:
                        halves_ready(pe, s, blk, "t2", b)
                    bank_free(pe, s, piece, b)
                    if name == "t1":
                        mm = transposes(bank, x_norm if blk == 0 else x_in_t, i)
                    elif name == "qk":
                        col = D * (i % 2) + P * (i // 2)
                        mm = products(bank[:, :], [(halves(w_qkv, c, slice(col, col + P)), halves(feat_a, c, every))
                                                   for c in range(DC)])
                    elif name == "v":
                        mm = products(bank[:, 0:D], [(halves(feat_a, c, tokens),
                                                      halves(w_qkv, c, slice(2 * D, 3 * D))) for c in range(DC)])
                    elif name == "t3":
                        mm = transposes(bank, attn, i)
                    elif name == "wout":
                        mm = products(bank[:, 0:D], [(halves(feat_m, c, tokens), halves(w_out, c, slice(0, D)))
                                                     for c in range(DC)])
                    elif name == "t2":
                        mm = transposes(bank, x_norm if blk == 0 else x_res, i)
                    else:
                        mm = products(bank[:, :], [(halves(w_up, c, tokens), halves(feat_m, c, every))
                                                   for c in range(DC)])
                    mm.then_inc(s["dense_ready"], 1)

                def scores(b, u, short, s=s):
                    g, half, j = u // 8, u // 4 % 2, u % 4
                    if u % 8 == 0:
                        loaded = (s["group0_loaded"], s["group1_loaded"])[g % 2]
                        after(pe, loaded, b, 2 * 9 * 16, (g // 2 + 1) * 9 * 16)
                    if short:
                        after(pe, s["scores_used"], b, TILES, max(2 * u, 2))
                        for i in range(2):
                            q0 = HALF * half + P * i
                            mm = pe.matmul(score_bank[u % 2][:, HALF * i:HALF * i + HALF],
                                           q_rows[:, g % 2, j, q0:q0 + P], k_rows[:, g % 2, j, L - HALF:L],
                                           start=True, stop=True)
                        mm.then_inc(s["scores_ready"], 2)
                        return
                    for i in range(2):
                        t = 2 * u + i
                        after(pe, s["scores_used"], b, TILES, t + 1)
                        q0 = HALF * half + P * i
                        pe.matmul(score_bank[t % 2][:, :], q_rows[:, g % 2, j, q0:q0 + P],
                                  k_rows[:, g % 2, j, :], start=True, stop=True).then_inc(s["scores_ready"], 1)

                def release_group(b, g, s=s):
                    after(pe, s["scores_ready"], b, TILES, 16 * (g + 1))
                    pe.sem_inc(s["group_used"], 1)

                def turn_unit(b, u, short, s=s):
                    if short:
                        after(pe, s["scores_used"], b, TILES, 2 * u + 2 + 2)
                        after(pe, s["probs_ready"], b, TILES, max(2 * u, 2))
                        for i in range(2):
                            mm = pe.transpose(turned_bank[u % 2][:, P * i:P * i + P], shifted[:, u % 3, i, 0:P],
                                              ident[:, :])
                        mm.then_inc(s["turned_ready"], 2)
                        return
                    after(pe, s["shifted_ready"], b, UNITS, u + 1)
                    for pair in range(2):
                        z = 2 * u + pair
                        after(pe, s["probs_ready"], b, TILES, z + 1)
                        for kk in range(2):
                            kt = 2 * pair + kk
                            for i in range(2):
                                mm = pe.transpose(turned_bank[z % 2][:, HALF * kk + P * i:HALF * kk + P * i + P],
                                                  shifted[:, u % 3, i, P * kt:P * kt + P], ident[:, :])
                        mm.then_inc(s["turned_ready"], 1)

                def attend(b, gq, key_tiles, short, s=s, blk=blk):
                    if gq == 0:
                        for t in [TT - 1] if short else key_tiles:
                            piece_read(pe, s, ("v", t), b)
                        if blk == 1 and key_tiles[0] == 0:
                            after(pe, s["vmask_ready"], b, 1, 1)
                    if key_tiles[0] == 0:
                        after(pe, s["probs_ready"], b, TILES, 8 * gq + 8 + 2)
                        after(pe, s["head_out_ready"], b, GQ, gq + 1)
                    for kt in key_tiles if not short else [TT - 1]:
                        for j in range(HG):
                            mm = pe.matmul(pv_bank[SLOT * j:SLOT * j + SLOT, 0:HALF],
                                           v_ext[:, kt, HG * (gq // 2) + j, :],
                                           probs[:, (4 * gq + j) % RING, kt, :], start=(kt == 0 or short), stop=(kt == TT - 1),
                                           skip_group_check=True)
                    if key_tiles[-1] == TT - 1:
                        mm.then_inc(s["probs_used"], 1)

                def to_tokens(b, gq, s=s):
                    after(pe, s["head_out_ready"], b, GQ, gq + 1 + 1)
                    after(pe, s["attn_ready"], b, GQ, gq + 2)
                    for i in range(2):
                        mm = pe.transpose(token_bank[:, P * i:P * i + P], head_out[:, gq % 2, P * i:P * i + P],
                                          ident[:, :])
                    mm.then_inc(s["token_ready"], 1)

                def turn(b, has_back, has_front, short, blk=blk):
                    for k in range(STEPS):
                        if k < UNITS:
                            scores(b, k, short)
                        if k >= 10 and (k - 10) % 8 == 0:
                            release_group(b, (k - 10) // 8)
                        for first, last, lag in ATTEND:
                            if k >= lag and (k - lag) % 4 == 0 and (k - lag) // 4 < GQ:
                                if not short:
                                    attend(b, (k - lag) // 4, range(first, last), False)
                                elif last == TT:
                                    attend(b, (k - lag) // 4, range(TT), True)
                        if TURN <= k < TURN + UNITS:
                            turn_unit(b, k - TURN, short)
                        if k >= OUT + 2 and (k - OUT - 2) % 4 == 0:
                            to_tokens(b, (k - OUT - 2) // 4)
                        for piece, of in pieces(blk, k, b, has_back, has_front):
                            dense(piece, of)
                        if has_back and k in DOWN_STEP[blk]:
                            down_chunks(b - 1, *DOWN_STEP[blk][k])
                    for gq in range(GQ):
                        if OUT + 2 + 4 * gq >= STEPS:
                            to_tokens(b, gq)

                def prologue(blk=blk):
                    for piece in ORDER[blk]:
                        if kind(piece) == 1:
                            dense(piece, 0)

                def epilogue(blk=blk):
                    for piece in ORDER[blk]:
                        if kind(piece) == -1:
                            dense(piece, B - 1)
                    down_chunks(B - 1, 0, TT * FCH)

                run(pe, blk, prologue, turn, epilogue)

        @block.scalar
        def _(act):
            def high_weights(blk):
                act.wait_ge(raw_loaded[blk], 16 * RAW_LOADS)
                for wide, raw_w in ((w_qkv, raw_qkv), (w_out, raw_out), (w_up, raw_up)):
                    act.activation(wide[:, 0, :, :], raw_w, ACT.Copy).then_inc(w_high[blk], 1)

            act.wait_ge(small_loaded, 16 * SMALL_LOADS)
            act.activation(cond_g[:, :, :], cond_t[:, :, :], ACT.Gelu_apprx_tanh).then_inc(cond_ready, 1)
            act.wait_ge(tp_ready, 2)
            for c in range(DC):
                act.activation(u_t[:, c, :], dense_bank[1][:, B * c:B * c + B], ACT.Silu,
                               bias=ada1_col[:, c:c + 1]).then_inc(silu_ready, 1)
            high_weights(0)
            act.wait_ge(w_loaded[0], 16 * W_LOADS)
            act.wait_ge(setup_done, 1)

            for blk, s in enumerate(S):
                if blk == 1:
                    act.wait_ge(w_loaded[blk], 16 * W_LOADS)

                def dense(piece, b, s=s, blk=blk):
                    name, i = piece
                    bank = dense_bank[bank_of(blk, piece)]
                    if name in ("t1", "t2", "t3"):
                        piece_ready(act, s, piece, b)
                        high = (feat_a if name == "t1" else feat_m)[:, 0, i, :]
                        if blk == 0 and name != "t3":
                            factor, offset = ((ab[:, x, i, bass.ds(b, 1)] if name == "t1" else ln2_gb[:, x, i:i + 1])
                                              for x in range(2))
                            act.activation(feat_tmp[:, i, :], bank[:, :], ACT.Identity, scale=factor, bias=offset)\
                                .then_inc(used(s, piece), 1)
                            piece_read(act, s, piece, b)
                            act.activation(high, feat_tmp[:, i, :], ACT.Copy).then_inc(s[name + "_high"], 1)
                        else:
                            act.activation(high, bank[:, :], ACT.Copy).then_inc(s[name + "_high"], 1)
                    elif name == "qk":
                        piece_ready(act, s, piece, b)
                        if i == 0:
                            after(act, s["base_free"], b, 1, 1)
                        act.activation(qk_high[:, i, :], bank[:, :], ACT.Copy,
                                       scale=QUERY_SCALE if i % 2 == 0 else 1.0).then_inc(s["qk_high"], 1)
                    elif name == "v":
                        if i == 0:
                            if blk == 1:
                                after(act, s["col_ready"], b, 1, 1)
                            after(act, s["probs_used"], b, GQ, 1)
                        piece_ready(act, s, piece, b)
                        act.activation(v_ext[:, i, :, 0:HD], bank[:, 0:D].rearrange("p (h e) -> p h e", h=H),
                                       ACT.Copy, scale=1.0 if blk == 0 else mask_colf[:, i:i + 1])\
                            .then_inc(used(s, piece), 1)
                    elif name == "up":
                        piece_ready(act, s, piece, b)
                        act.activation(hidden[:, i, :], bank[:, :], ACT.Gelu_apprx_tanh if blk == 0 else ACT.Gelu,
                                       bias=up_bias[:, i:i + 1]).then_inc(used(s, piece), 1)

                def make_bias(b, u, s=s):
                    g, half, j = u // 8, u // 4 % 2, u % 4
                    h = HG * g + j
                    after(act, s["bias_used"], b, UNITS, u + 1)
                    act.activation(bias[:, u % 2, :, :], dist[:, 2 * half:2 * half + 2, :], ACT.Copy,
                                   scale=neg_scale[:, h:h + 1]).then_inc(s["bias_ready"], 1)

                def exps(b, u, short, s=s):
                    if u == 0:
                        after(act, s["probs_used"], b, GQ, 1)
                    elif u >= RING and (u - RING) % HG == 0:
                        after(act, s["probs_used"], b, GQ, 1 + (u - RING) // HG + 1)
                    if short:
                        after(act, s["turned_ready"], b, TILES, 2 * u + 2)
                        act.activation(probs[:, u % RING, TT - 1, :], turned_bank[u % 2][:, 0:HALF], ACT.Exp)\
                            .then_inc(s["probs_ready"], 2)
                        return
                    for pair in range(2):
                        z = 2 * u + pair
                        after(act, s["turned_ready"], b, TILES, z + 1)
                        act.activation(probs[:, u % RING, 2 * pair:2 * pair + 2, :],
                                       turned_bank[z % 2][:, :].rearrange("p (a c) -> p a c", a=2), ACT.Exp)\
                            .then_inc(s["probs_ready"], 1)

                def take_out(b, gq, s=s):
                    after(act, s["probs_used"], b, GQ, gq + 1 + 1)
                    after(act, s["attn_ready"], b, GQ, gq + 1)
                    act.activation(head_out[:, gq % 2, :], pv_bank[:, 0:HALF], ACT.Copy)\
                        .then_inc(s["head_out_ready"], 1)

                def turn(b, has_back, has_front, short, blk=blk):
                    if blk == 0:
                        make_bias(b, 0)
                        make_bias(b, 1)
                    for k in range(STEPS):
                        if k >= OUT and (k - OUT) % 4 == 0:
                            take_out(b, (k - OUT) // 4)
                        for piece, of in pieces(blk, k, b, has_back, has_front):
                            dense(piece, of)
                        if blk == 0 and k + 2 < UNITS:
                            make_bias(b, k + 2)
                        if 1 <= k <= UNITS:
                            exps(b, k - 1, short)
                    for gq in range(GQ):
                        if OUT + 4 * gq >= STEPS:
                            take_out(b, gq)

                def prologue(blk=blk):
                    for piece in ORDER[blk]:
                        if kind(piece) == 1:
                            dense(piece, 0)

                def epilogue(blk=blk):
                    for piece in ORDER[blk]:
                        if kind(piece) == -1:
                            dense(piece, B - 1)
                            if blk == 0 and piece == ("up", FCH - 1):
                                high_weights(1)

                run(act, blk, prologue, turn, epilogue)

        @block.vector
        def _(dve):
            steps = 0

            def step(ins):
                nonlocal steps
                steps += 1
                ins.then_inc(setup_step, 1)
                dve.wait_ge(setup_step, steps)

            def low_weights(blk):
                for n, (wide, raw_w) in enumerate(((w_qkv, raw_qkv), (w_out, raw_out), (w_up, raw_up))):
                    dve.wait_ge(w_high[blk], n + 1)
                    dve.tensor_tensor(wide[:, 1, :, :], raw_w, wide[:, 0, :, :].bitcast(F32), ALU.subtract)\
                        .then_inc(w_split[blk], 1)

            dve.memset(no_bias[:, :], 0.0).then_inc(dve_consts, 1)
            step(dve.memset(v_ext[:, :, :, :], 0.0))
            dve.memset(v_ext[:, :, :, HD], 1.0).then_inc(dve_consts, 1)
            dve.memset(q_rows[KROWS:KROWS + 1, :, :, :].bitcast(F32), 1.0).then_inc(dve_consts, 1)
            for s in S:
                for name, n in (("base_free", 1), ("group_used", 2), ("scores_used", 2), ("bias_used", 2),
                                ("probs_ready", 2), ("probs_used", 1), ("head_out_ready", 1), ("attn_ready", 2),
                                ("dense_used0", 1), ("dense_used1", 1), ("y_ready", 1), ("y_stored", 16)):
                    dve.sem_inc(s[name], n)
            dve.wait_ge(small_loaded, 16 * SMALL_LOADS)
            step(dve.tensor_scalar_mul(neg_scale[:, :], neg_scale[:, :], -1.0))
            dve.wait_ge(tp_ready, 1)
            step(dve.tensor_tensor(tp[:, :, :], dense_bank[0][:, 0:4 * B].rearrange("p (c b) -> p c b", c=4),
                                   bt_col[:, :].unsqueeze(2).broadcast_to([P, 4, B]), ALU.add))
            step(dve.tensor_scalar_add(tp[:, 0:2, :], tp[:, 0:2, :], 1.0))
            step(dve.tensor_tensor(ab[:, 0, :, :], tp[:, 0:2, :],
                                   ln1_gb[:, 0, :].unsqueeze(2).broadcast_to([P, DC, B]), ALU.mult))
            step(dve.tensor_tensor(ab[:, 1, :, :], tp[:, 0:2, :],
                                   ln1_gb[:, 1, :].unsqueeze(2).broadcast_to([P, DC, B]), ALU.mult))
            step(dve.tensor_tensor(ab[:, 1, :, :], ab[:, 1, :, :], tp[:, 2:4, :], ALU.add))
            low_weights(0)
            for c in range(3):
                dve.wait_ge(ada_ready, c + 1)
                bank = (score_bank[0], score_bank[1], turned_bank[0])[c]
                step(dve.tensor_tensor(ada[:, L * c:L * c + L], bank[0:B, :], ada2_bias[:, L * c:L * c + L], ALU.add))
            for n in range(2):
                shift, scale, gate = (ada[:, (3 * n + m) * D:(3 * n + m + 1) * D] for m in range(3))
                step(dve.scalar_tensor_tensor(out=mod_out[:, 2 * n * D:(2 * n + 1) * D], in0=scale, scalar=1.0,
                                              in1=gate, op0=ALU.add, op1=ALU.mult))
                step(dve.tensor_tensor(mod_out[:, (2 * n + 1) * D:(2 * n + 2) * D], shift, gate, ALU.mult))
            step(dve.tensor_reduce(early_max[:, :], all_masks[:, :, 0:EARLY], mybir.AxisListType.X, ALU.max))
            step(dve.tensor_copy(early_flag[:, :], early_max[:, :]))
            assert steps == SETUP_STEPS
            dve.wait_ge(setup_done, 1)

            for blk, s in enumerate(S):
                def norm_stats(b, n, src, s=s):
                    for t in range(TT):
                        ins = dve.bn_stats(stats[:, n, t, :], src[:, t, :])
                    ins.then_inc(s[f"stats_ready{n}"], 1)
                    after_alone(dve, s[f"stats_ready{n}"], b, 1, 1)
                    for t in range(TT):
                        ins = dve.bn_aggr(mean_var[:, n, t, :], stats[:, n, t, :])
                    ins.then_inc(s[f"mean_ready{n}"], 1)

                def norm_apply(b, n, src, s=s):
                    after(dve, s[f"rstd_ready{n}"], b, 1, 1)
                    for t in range(TT):
                        ins = dve.tensor_scalar(x_norm[:, t, :], src[:, t, :], mean_var[:, n, t, 0:1],
                                                rstd[:, n, t:t + 1], ALU.subtract, ALU.mult)
                    ins.then_inc(s[f"norm_ready{n}"], 1)

                def modulate(b, n, out_t, done, s=s):
                    after(dve, s[f"norm_ready{n}"], b, 1, 1)
                    dve.tensor_tensor(x_norm[:, :, :], x_norm[:, :, :],
                                      mod[:, 2 * n:2 * n + 1, :].broadcast_to([P, TT, D]), ALU.mult)\
                        .then_inc(s["scaled"], 1)
                    after(dve, s["scaled"], b, 2, n + 1)
                    after(dve, s[f"res_ready{n}"], b, 1, 1)
                    dve.tensor_tensor(out_t, x_norm[:, :, :], x_res[:, :, :], ALU.add).then_inc(s[done], 1)

                def norm(what, n, b, s=s, blk=blk):
                    if blk == 0 and n == 0:
                        if what == "stats":
                            after(dve, s["x_loaded"], b, 16, 16)
                            norm_stats(b, 0, x_in_t)
                        else:
                            if not isinstance(b, int) or b > 1:
                                after(dve, s["y_stored"], b, 16, -16)
                            norm_apply(b, 0, x_in_t)
                    elif blk == 0:
                        if what == "stats":
                            for t in range(2):
                                piece_read(dve, s, ("wout", 2 + t), b)
                            norm_stats(b, 1, x_res)
                        else:
                            if isinstance(b, int) and b + 2 >= B:
                                after(dve, s["y_stored"], b, 16, 16)
                            else:
                                piece_ready(dve, s, ("t1", DC - 1), b + 2)
                            norm_apply(b, 1, x_res)
                    elif n == 0:
                        if what == "stats":
                            for t in range(2):
                                piece_read(dve, s, ("wout", 2 + t), b)
                            norm_stats(b, 0, branch)
                        else:
                            after(dve, s["y_stored"], b, 16, 16)
                            norm_apply(b, 0, branch)
                            modulate(b, 0, x_res[:, :, :], "mid_ready")
                    else:
                        if what == "stats":
                            for t in range(2):
                                piece_read(dve, s, ("down", 2 + t), b)
                            norm_stats(b, 1, branch)
                        else:
                            norm_apply(b, 1, branch)
                            modulate(b, 1, x_norm[:, :, :], "y_ready")

                def dense(piece, b, s=s, blk=blk):
                    name, i = piece
                    bank = dense_bank[bank_of(blk, piece)]
                    if name in ("t1", "t2", "t3"):
                        after(dve, s[name + "_high"], b, DC, i + 1)
                        feat = feat_a if name == "t1" else feat_m
                        if blk == 0 and name != "t3":
                            dve.tensor_tensor(feat[:, 1, i, :], feat_tmp[:, i, :], feat[:, 0, i, :].bitcast(F32),
                                              ALU.subtract).then_inc(s[name + "_low"], 1)
                        else:
                            dve.tensor_tensor(feat[:, 1, i, :], bank[:, :], feat[:, 0, i, :].bitcast(F32),
                                              ALU.subtract).then_inc(used(s, piece), 1)
                    elif name == "qk":
                        after(dve, s["qk_high"], b, 4, i + 1)
                        dve.scalar_tensor_tensor(out=qk_low[:, i, :], in0=bank[:, :],
                                                 scalar=QUERY_SCALE if i % 2 == 0 else 1.0,
                                                 in1=qk_high[:, i, :].bitcast(F32), op0=ALU.mult,
                                                 op1=ALU.subtract).then_inc(used(s, piece), 1)
                    elif name == "wout":
                        if i == 0 and blk == 0:
                            after(dve, s["res_loaded"], b, 16, 16)
                        piece_ready(dve, s, piece, b)
                        dst, other = (x_res[:, i, :], x_res[:, i, :]) if blk == 0 else (branch[:, i, :], out_bias[:, :])
                        dve.tensor_tensor(dst, other, bank[:, 0:D], ALU.add).then_inc(used(s, piece), 1)
                    elif name == "down":
                        if i == 0 and blk == 0:
                            after(dve, s["res_ready1"], b, 1, 1)
                        piece_ready(dve, s, piece, b)
                        dst, other = (x_norm[:, i, :], x_res[:, i, :]) if blk == 0 else (branch[:, i, :], down_bias[:, :])
                        dve.tensor_tensor(dst, other, bank[:, 0:D], ALU.add).then_inc(used(s, piece), 1)
                        if i == TT - 1 and blk == 0:
                            for t in range(2):
                                piece_read(dve, s, ("down", 2 + t), b)
                            dve.sem_inc(s["y_ready"], 1)

                def shift_scores(b, u, short, s=s, blk=blk):
                    if short:
                        heads = score_bank[u % 2][:, :].rearrange("p (i k) -> p i k", i=2)[:, :, HALF - P:HALF]
                        peak = row_max[:, 2 * (u % 2):2 * (u % 2) + 2]
                        after(dve, s["scores_ready"], b, TILES, 2 * u + 2)
                        dve.tensor_reduce(peak, heads, mybir.AxisListType.X, ALU.max).then_inc(s["bias_used"], 1)
                        after(dve, s["bias_used"], b, UNITS, u + 1 + 2)
                        dve.tensor_tensor(shifted[:, u % 3, :, 0:P], heads,
                                          peak.unsqueeze(2).broadcast_to([P, 2, P]), ALU.subtract)\
                            .then_inc(s["scores_used"], 2)
                        dve.sem_inc(s["shifted_ready"], 1)
                        return
                    if blk == 0:
                        after(dve, s["bias_ready"], b, UNITS, u + 1)
                    for i in range(2):
                        t = 2 * u + i
                        after_alone(dve, s["scores_ready"], b, TILES, t + 1)
                        dve.tensor_tensor_reduce(shifted[:, u % 3, i, :], score_bank[t % 2][:, :],
                                                 bias[:, u % 2, i, :] if blk == 0 else no_bias[:, :],
                                                 1.0, -3.0e38, ALU.add, ALU.max, row_max[:, t % 4:t % 4 + 1])\
                            .then_inc(s["scores_used"], 1)
                    for i in range(2):
                        t = 2 * u + i
                        after(dve, s["scores_used"], b, TILES, t + 1 + 2)
                        ins = dve.tensor_scalar(shifted[:, u % 3, i, :], shifted[:, u % 3, i, :],
                                                row_max[:, t % 4:t % 4 + 1], None, ALU.subtract)
                        ins.then_inc(s["bias_used"] if i == 0 else s["shifted_ready"], 1)

                def divide(b, gq, s=s):
                    after(dve, s["token_ready"], b, GQ, gq + 1)
                    heads = token_bank[:, 0:2 * P].rearrange("p (i j e) -> p i j e", i=2, e=SLOT)
                    dve.reciprocal(inv_sum[:, :, :], heads[:, :, :, HD]).then_inc(s["inv_ready"], 1)
                    after(dve, s["inv_ready"], b, GQ, gq + 1)
                    g, t0 = gq // 2, 2 * (gq % 2)
                    for i in range(2):
                        ins = dve.tensor_tensor(attn[:, t0 + i, HG * HD * g:HG * HD * (g + 1)]
                                                .rearrange("p (j e) -> p j e", j=HG), heads[:, i, :, 0:HD],
                                                inv_sum[:, i, :].unsqueeze(2).broadcast_to([P, HG, HD]), ALU.mult)
                    ins.then_inc(s["attn_ready"], 1)

                def turn(b, has_back, has_front, short, blk=blk, s=s):
                    for k in range(STEPS):
                        if k < UNITS:
                            shift_scores(b, k, short)
                        if k >= OUT + 3 and (k - OUT - 3) % 4 == 0:
                            if k == OUT + 3 and has_back:
                                piece_ready(dve, s, ("t3", DC - 1), b - 1)
                            divide(b, (k - OUT - 3) // 4)
                        for piece, of in pieces(blk, k - 1, b, has_back, has_front):
                            dense(piece, of)
                        for what, n in NORM_STEP[blk].get(k, []):
                            ahead = blk == 0 and n == 0
                            if has_front if ahead else has_back:
                                norm(what, n, b + 1 if ahead else b - 1)
                    for gq in range(GQ):
                        if OUT + 3 + 4 * gq >= STEPS:
                            divide(b, gq)
                    for piece, of in pieces(blk, STEPS - 1, b, has_back, has_front):
                        dense(piece, of)
                    if has_back:
                        for what, n in NORM_STEP[blk].get(STEPS, []):
                            norm(what, n, b - 1)

                def prologue(blk=blk):
                    if blk == 0:
                        norm("stats", 0, 0)
                        norm("norm", 0, 0)
                    for piece in ORDER[blk]:
                        if kind(piece) == 1:
                            dense(piece, 0)

                def epilogue(blk=blk):
                    for piece in ORDER[blk]:
                        if kind(piece) == -1:
                            dense(piece, B - 1)
                            if blk == 0 and piece == ("up", FCH - 1):
                                low_weights(1)
                            if piece == ("wout", TT - 1):
                                n = 1 if blk == 0 else 0
                                norm("stats", n, B - 1)
                                norm("norm", n, B - 1)
                    if blk == 1:
                        norm("stats", 1, B - 1)
                        norm("norm", 1, B - 1)

                run(dve, blk, prologue, turn, epilogue)


SMALL_LOADS = 15
POOL_CONSTS = 3
DVE_CONSTS = 3
SETUP_STEPS = 2 + 5 + 3 + 4 + 2

_INS = ['x', 'cond_1024', 'mask_BxS_bf1', 'mask_BxS_bk0', 'L0_cond_torus_dist', 'L0_cond_ln1_g', 'L0_cond_ln1_b',
        'L0_cond_Wqkv', 'L0_cond_Wout', 'L0_cond_torus_scale', 'L0_cond_ln2_g', 'L0_cond_ln2_b', 'L0_cond_W1',
        'L0_cond_b1', 'L0_cond_W2', 'L0_cond_b2', 'L0_cond_Wt', 'L0_cond_bt', 'L1_cond_qkv_w', 'L1_cond_proj_w',
        'L1_cond_proj_b', 'L1_cond_fc1_w', 'L1_cond_fc1_b', 'L1_cond_fc2_w', 'L1_cond_fc2_b', 'L1_cond_ada1_w',
        'L1_cond_ada1_b', 'L1_cond_ada2_w', 'L1_cond_ada2_b']


def kernel(**inputs):
    import numpy as np
    import concourse.bacc as bacc
    from concourse.bass_utils import run_bass_kernel_spmd

    nc = bacc.Bacc("TRN2", target_bir_lowering=False, num_devices=1)
    arrays, d = {}, {}
    for name in _INS:
        a = np.ascontiguousarray(inputs[name])
        arrays[f"in_{name}"] = a
        d[name] = nc.dram_tensor(f"in_{name}", a.shape, mybir.dt.from_np(a.dtype), kind="ExternalInput").ap()
    out = nc.dram_tensor("out", inputs["x"].shape, F32, kind="ExternalOutput").ap()
    build(nc, d, out)
    r = run_bass_kernel_spmd(nc, [arrays], core_ids=[0])
    return r.results[0]["out"]
```
